# Optimizing a Trainium2 kernel written in Bass

```python
import numpy as np
import jax
import jax.numpy as jnp

def _softmax(x, axis=-1):
    return jax.nn.softmax(x, axis=axis)

def _gelu(x):
    return jax.nn.gelu(x, approximate=True)

def _silu(x):
    return jax.nn.silu(x)

def _sigmoid(x):
    return jax.nn.sigmoid(x)

def _layernorm(x, axis=-1, eps=1e-05):
    m = jnp.mean(x, axis=axis, keepdims=True)
    v = jnp.var(x, axis=axis, keepdims=True)
    return (x - m) / jnp.sqrt(v + eps)

def _scatter_add(tgt, idx, src, axis=0):
    return tgt.at[idx].add(src)

def _segment_sum(src, seg, n):
    return jax.ops.segment_sum(src, seg, n)
kernel_name = 'mk_flamingo_gated_d1_seqx_r4_45ca6b'

def setup_inputs(seed: int=0):
    np.random.seed(seed)
    _w = jnp.asarray

    def _rec_inputs():
        import jax
        import jax.numpy as jnp
        _rk = jax.random.key(seed)
        x = -0.0002928 + 1 * jax.random.normal(jax.random.fold_in(_rk, 1), (4, 512, 512), jnp.float32)
        _lenS = 512 - jax.random.randint(jax.random.fold_in(_rk, 7), (4,), 0, max(1, 512 // 4) + 1, jnp.int32)
        _lenS2 = 64 - jax.random.randint(jax.random.fold_in(_rk, 8), (4,), 0, max(1, 64 // 4) + 1, jnp.int32)
        _ctx_512P = jax.random.normal(jax.random.fold_in(_rk, 11), (4, 16, 128), jnp.float32)
        _ctx_512c = jax.random.dirichlet(jax.random.fold_in(_rk, 511), 0.3 * jnp.ones((16,), jnp.float32), (4, 64))
        _ctx_512t = jnp.einsum('bsk,bkd->bsd', _ctx_512c, _ctx_512P)
        _ctx_512t = _ctx_512t * jax.lax.rsqrt(jnp.mean(jnp.square(_ctx_512t)) + 1e-12) * 0.953939
        ctx_512 = 0.000227908 + 0.99994 * (_ctx_512t + 0.3 * jax.random.normal(jax.random.fold_in(_rk, 611), (4, 64, 128), jnp.float32))
        _g = jax.random.normal(jax.random.fold_in(_rk, 9001), (2, 1), jnp.float32)
        _g = jnp.sign(_g) * jnp.maximum(jnp.abs(_g), 1.0) + (_g == 0) * 1.0
        g_xattn = _g[0]
        g_ffn = _g[1]
        return (x, ctx_512, g_xattn, g_ffn)
    x, ctx_512, g_xattn, g_ffn = _rec_inputs()

    def _L0_xattn_setup():
        import jax, jax.numpy as jnp
        import numpy as np
        B, S, L = (2, 256, 256)
        DIM_Q, H, K, D_C, D_CQ, R = (512, 16, 128, 128, 384, 64)

        def _rope_tables(seq_len, dim, dtype):
            inv_freq = 1.0 / 10000.0 ** (jnp.arange(0, dim, 2, dtype=dtype) / dim)
            t = jnp.arange(seq_len, dtype=dtype)
            freqs = t[:, None] * inv_freq[None, :]
            sin = jnp.repeat(jnp.sin(freqs), 2, axis=-1)
            cos = jnp.repeat(jnp.cos(freqs), 2, axis=-1)
            return (sin, cos)

        def _rotate_half(x):
            h = x.shape[-1] // 2
            return jnp.concatenate([-x[..., h:], x[..., :h]], axis=-1)
        key = jax.random.key(seed)
        ks = jax.random.split(key, 8)
        s_in = 1.0 / np.sqrt(DIM_Q)
        s_k = 1.0 / np.sqrt(K)
        s_cq = 1.0 / np.sqrt(D_CQ)
        s_c = 1.0 / np.sqrt(D_C)
        return {'hidden_q': jax.random.normal(ks[0], (B, S, DIM_Q), jnp.float32), 'kv_c': jax.random.normal(ks[1], (B, L, D_C), jnp.float32), 'Wq': jax.random.normal(ks[2], (H * K, DIM_Q), jnp.float32) * s_in, 'w_kc_q': jax.random.normal(ks[3], (H, K, D_CQ), jnp.float32) * s_k, 'w_kc_kv': jax.random.normal(ks[4], (H, K, D_C), jnp.float32) * s_k, 'W_qr': jax.random.normal(ks[5], (H, D_CQ, R), jnp.float32) * s_cq / np.sqrt(R), 'W_kr': jax.random.normal(ks[6], (H, D_C, R), jnp.float32) * s_c, 'Wo': jax.random.normal(ks[7], (DIM_Q, H * K), jnp.float32) * s_k}
    _L0_xattn_all = _L0_xattn_setup()
    _L0_xattn_in = {k: v for k, v in _L0_xattn_all.items() if k in ('Wq', 'w_kc_q', 'w_kc_kv', 'W_qr', 'W_kr', 'Wo')}
    del _L0_xattn_all

    def _L0_ffn_setup():
        import jax, jax.numpy as jnp
        import numpy as np
        DIM = 512
        HID = 1408
        ZERO_POINT = 128.0

        def _qlinear(x, wq, scale):
            W = (wq.astype(jnp.float32) - ZERO_POINT) * scale[:, None]
            return jnp.einsum('bsd,hd->bsh', x, W)
        key = jax.random.key(seed)
        ks = jax.random.split(key, 7)
        B, S = (4, 512)
        sg = jax.random.uniform(ks[1], (HID,)) * (0.02 / np.sqrt(DIM)) + 0.0001
        su = jax.random.uniform(ks[3], (HID,)) * (0.02 / np.sqrt(DIM)) + 0.0001
        sd = jax.random.uniform(ks[5], (DIM,)) * (0.02 / np.sqrt(HID)) + 0.0001
        return {'x': jax.random.normal(ks[0], (B, S, DIM), dtype=jnp.float32), 'wq_gate': jax.random.randint(ks[2], (HID, DIM), 0, 64, dtype=jnp.int32), 's_gate': sg, 'wq_up': jax.random.randint(ks[4], (HID, DIM), 0, 64, dtype=jnp.int32), 's_up': su, 'wq_down': jax.random.randint(ks[6], (DIM, HID), 0, 64, dtype=jnp.int32), 's_down': sd}
    _L0_ffn_all = _L0_ffn_setup()
    _L0_ffn_in = {k: v for k, v in _L0_ffn_all.items() if k in ('wq_gate', 's_gate', 'wq_up', 's_up', 'wq_down', 's_down')}
    del _L0_ffn_all
    return {'x': x, 'ctx_512': ctx_512, 'g_xattn': g_xattn, 'g_ffn': g_ffn, 'L0_xattn_Wq': _L0_xattn_in['Wq'], 'L0_xattn_w_kc_q': _L0_xattn_in['w_kc_q'], 'L0_xattn_w_kc_kv': _L0_xattn_in['w_kc_kv'], 'L0_xattn_W_qr': _L0_xattn_in['W_qr'], 'L0_xattn_W_kr': _L0_xattn_in['W_kr'], 'L0_xattn_Wo': _L0_xattn_in['Wo'], 'L0_ffn_wq_gate': _L0_ffn_in['wq_gate'], 'L0_ffn_s_gate': _L0_ffn_in['s_gate'], 'L0_ffn_wq_up': _L0_ffn_in['wq_up'], 'L0_ffn_s_up': _L0_ffn_in['s_up'], 'L0_ffn_wq_down': _L0_ffn_in['wq_down'], 'L0_ffn_s_down': _L0_ffn_in['s_down']}

def reference(x, ctx_512, g_xattn, g_ffn, L0_xattn_Wq, L0_xattn_w_kc_q, L0_xattn_w_kc_kv, L0_xattn_W_qr, L0_xattn_W_kr, L0_xattn_Wo, L0_ffn_wq_gate, L0_ffn_s_gate, L0_ffn_wq_up, L0_ffn_s_up, L0_ffn_wq_down, L0_ffn_s_down):
    import jax
    import jax.numpy as jnp

    def _L0_xattn_ref(hidden_q, kv_c, Wq, w_kc_q, w_kc_kv, W_qr, W_kr, Wo):
        import jax, jax.numpy as jnp
        import numpy as np
        B, S, L = (2, 256, 256)
        DIM_Q, H, K, D_C, D_CQ, R = (512, 16, 128, 128, 384, 64)

        def _rope_tables(seq_len, dim, dtype):
            inv_freq = 1.0 / 10000.0 ** (jnp.arange(0, dim, 2, dtype=dtype) / dim)
            t = jnp.arange(seq_len, dtype=dtype)
            freqs = t[:, None] * inv_freq[None, :]
            sin = jnp.repeat(jnp.sin(freqs), 2, axis=-1)
            cos = jnp.repeat(jnp.cos(freqs), 2, axis=-1)
            return (sin, cos)

        def _rotate_half(x):
            h = x.shape[-1] // 2
            return jnp.concatenate([-x[..., h:], x[..., :h]], axis=-1)
        b, s, _ = hidden_q.shape
        l = kv_c.shape[1]
        q_hk = (hidden_q @ Wq.T).reshape(b, s, H, K)
        q_big = jnp.einsum('bshk,hkq->bshq', q_hk, w_kc_q)
        sin, cos = _rope_tables(l, D_C, kv_c.dtype)
        kv_rope = kv_c * cos[None] + _rotate_half(kv_c) * sin[None]
        q_r = jnp.einsum('bshq,hqr->bhsr', q_big, W_qr)
        k_r = jnp.einsum('bld,hdr->bhlr', kv_rope, W_kr)
        scores = jnp.einsum('bhsr,bhlr->bhsl', q_r, k_r)
        attn = jax.nn.softmax(scores, axis=-1)
        ctx_c = jnp.einsum('bhsl,bld->bhsd', attn, kv_rope)
        ctx_lat = jnp.einsum('bhsd,hkd->bshk', ctx_c, w_kc_kv)
        out = ctx_lat.reshape(b, s, H * K) @ Wo.T
        return out

    def _L0_ffn_ref(x, wq_gate, s_gate, wq_up, s_up, wq_down, s_down):
        import jax, jax.numpy as jnp
        import numpy as np
        DIM = 512
        HID = 1408
        ZERO_POINT = 128.0

        def _qlinear(x, wq, scale):
            W = (wq.astype(jnp.float32) - ZERO_POINT) * scale[:, None]
            return jnp.einsum('bsd,hd->bsh', x, W)
        gate = _qlinear(x, wq_gate, s_gate)
        gate = jax.nn.silu(gate)
        up = _qlinear(x, wq_up, s_up)
        return _qlinear(gate * up, wq_down, s_down)
    x = x + jnp.tanh(g_xattn[0]) * _L0_xattn_ref(_layernorm(x, axis=-1), ctx_512, L0_xattn_Wq, L0_xattn_w_kc_q, L0_xattn_w_kc_kv, L0_xattn_W_qr, L0_xattn_W_kr, L0_xattn_Wo)
    x = x + jnp.tanh(g_ffn[0]) * _L0_ffn_ref(_layernorm(x, axis=-1), L0_ffn_wq_gate, L0_ffn_s_gate, L0_ffn_wq_up, L0_ffn_s_up, L0_ffn_wq_down, L0_ffn_s_down)
    return x

_drawn_inputs = setup_inputs


def setup_inputs(seed=0):
    import zlib

    import numpy as np

    out = dict(_drawn_inputs(seed))
    spreads = {}
    factors = {'L0_ffn_s_gate': 4.84, 'L0_ffn_s_up': 5.788, 'L0_ffn_s_down': 4.833}
    for name, (base, spread) in spreads.items():
        noise = np.random.default_rng([zlib.crc32(name.encode()), seed]).standard_normal(out[name].shape)
        drawn = base * np.exp(spread * noise) if base else spread * noise
        out[name] = jnp.asarray(drawn.astype(out[name].dtype))
    for name, factor in factors.items():
        out[name] = (out[name] * factor).astype(out[name].dtype)
    return out
```

```python
import concourse.bass as bass
from concourse import mybir
from contextlib import ExitStack

FP32 = mybir.dt.float32
FP16 = mybir.dt.float16
INT32 = mybir.dt.int32
ALU = mybir.AluOpType
ACT = mybir.ActivationFunctionType
AX = mybir.AxisListType
RMAX = bass.bass_isa.ReduceOp.max

P = 128
B, S, D = 4, 512, 512
H, L = 16, 64
DK = 128
DC = 128
CQ = 384
R = 64
HID = 1408
DCH = D // P
QCH = CQ // P
JCH = HID // P
TPB = S // P
NT = B * TPB
PAIRS = H // 2
BL = B * L
HL = H * L
EPS = 1e-5
ZERO_POINT = 128.0

X_SCALE = 256.0
P_SCALE = 4096.0
TOP = 32768.0
EXACT = 2048.0
TINY = 1e-30

DOWN_J = (3, 3, 3, 2)
PIECES = 3 * 4
HOLE = 3 * 1024


def down_piece(j):
    return j // DOWN_J[0], j % DOWN_J[0]


def piece_width(n):
    return HID if n < 8 else DOWN_J[n - 8] * D


def t2_at(h):
    return (h // 4) * 4 + (h % 2) * 2 + (h // 2) % 2


def gated_block(nc, x_d, ctx_d, ctx_swapped_d, cos_d, sin_d, gx_d, gf_d, wq_d, wkcq_d, wkckv_d,
                wqr_d, wkr_d, wo_d, wg_d, wu_d, wd_d, sg_d, su_d, sd_d, out_d):
    ctx = ExitStack()
    with ctx:
        def sb(name, shape, dt):
            return ctx.enter_context(nc.sbuf_tensor(name, shape, dt))

        def sem(name):
            return ctx.enter_context(nc.semaphore(name))

        g_region = sb("g_region", [P, 2 * DCH * B * HL], FP16)
        v_region = sb("v_region", [P, PAIRS * 2 * B * D], FP16)
        x_res = sb("x_res", [P, NT, D], FP32)
        work = sb("work", [P, 8192], FP32)
        ident = sb("ident", [P, P], FP32)
        kvt = sb("kvt", [P, BL], FP32)
        down_row = sb("down_row", [P, D], FP32)
        sg = sb("sg", [P, JCH], FP32)
        su = sb("su", [P, JCH], FP32)
        sgsu = sb("sgsu", [P, JCH], FP32)
        gx = sb("gx", [P, 1], FP32)
        gf = sb("gf", [P, 1], FP32)
        stats = sb("stats", [P, NT, 6], FP32)
        meanvar = sb("meanvar", [P, NT, 2], FP32)
        ln_scale = sb("ln_scale", [P, NT], FP32)
        ln_bias = sb("ln_bias", [P, NT], FP32)
        newton = sb("newton", [P, 4, NT], FP32)
        row_max = sb("row_max", [P, 2, H], FP32)
        row_sum = sb("row_sum", [P, 2, H], FP32)
        row_inv = sb("row_inv", [P, 2, H], FP32)
        part_max = sb("part_max", [P, 20], FP32)
        tens_max = sb("tens_max", [P, 8], FP32)
        all_max = sb("all_max", [P, 8], FP32)
        ffn_max = sb("ffn_max", [P, PIECES], FP32)
        sc = sb("sc", [P, 32], FP32)
        big = sb("big", [P, 1], INT32)

        g_all = g_region[:, :].rearrange("p (s c b n) -> p s c b n", s=2, c=DCH, b=B)
        v_all = v_region[:, :].rearrange("p (q s b n) -> p q s b n", q=PAIRS, s=2, b=B)
        g32 = g_region[:, :].bitcast(FP32)
        at = 0
        wkcq = g32[:, at:at + H * QCH * DK].rearrange("p (h c k) -> p h c k", h=H, c=QCH)
        at += H * QCH * DK
        wqr = g32[:, at:at + H * QCH * R].rearrange("p (h c r) -> p h c r", h=H, c=QCH)
        at += H * QCH * R
        wkr = g32[:, at:at + H * R]
        at += H * R
        wkckv = g32[:, at:at + H * DK]
        at += H * DK
        ctx_t = g32[:, at:at + BL]
        ctx_s = g32[:, at + BL:at + 2 * BL]
        cos_t = g32[:, at + 2 * BL:at + 2 * BL + L]
        sin_t = g32[:, at + 2 * BL + L:at + 2 * BL + 2 * L]
        v32 = v_region[:, :].bitcast(FP32)
        wq = v32[:, 0:H * D].rearrange("p (h n) -> p h n", h=H)
        wo = v32[:, H * D:2 * H * D].rearrange("p (h n) -> p h n", h=H)

        t2 = work[:, 0:H * BL]
        ex = [work[:, i * HL:(i + 1) * HL] for i in range(2)]
        xn = [work[:, 2048 + i * D:2048 + (i + 1) * D] for i in range(2)]
        xt = work[:, 3072:4096].bitcast(FP16).rearrange("p (i s c t) -> p i s c t", i=2, s=2, c=DCH)
        x2t = work[:, 0:2048].bitcast(FP16).rearrange("p (s c t) -> p s c t", s=2, c=DCH)
        xn2 = [work[:, 2048 + i * D:2048 + (i + 1) * D] for i in range(TPB)]
        krt = work[:, 4096:4096 + PAIRS * BL].rearrange("p (q n) -> p q n", q=PAIRS)
        a1t = work[:, 6144:6144 + PAIRS * DK].rearrange("p (q k) -> p q k", q=PAIRS)
        u_t = work[:, 4096:8192]
        pt = work[:, 4096:6144].bitcast(FP16).rearrange("p (i s q t) -> p i s q t", i=2, s=2, q=PAIRS)
        sil = [work[:, 4096 + i * S:4096 + (i + 1) * S] for i in range(2)]
        hid = [work[:, 5120 + i * S:5120 + (i + 1) * S] for i in range(2)]
        o_sb = [work[:, 6144 + i * D:6144 + (i + 1) * D] for i in range(TPB)]

        def hole(k):
            return g_region[:, k * B * HL:k * B * HL + HOLE]

        def w_hi(n):
            w = piece_width(n)
            return hole(n // 2)[:, (n % 2) * (HOLE // 2):(n % 2) * (HOLE // 2) + w]

        def staged(n):
            return hole(6 + n % 2).bitcast(INT32)[:, 0:piece_width(n)]

        def w_lo(n):
            return v_region[:, n * (HOLE // 2):n * (HOLE // 2) + piece_width(n)]

        widest = HOLE // 2
        h_all = v_region[:, PIECES * widest:PIECES * widest + 2 * JCH * S] \
            .rearrange("p (s j t) -> p s j t", s=2, j=JCH)
        w_tmp = v_region[:, PIECES * widest + 2 * JCH * S:PIECES * widest + 2 * JCH * S + 2 * widest].bitcast(FP32)

        ffn_src = [wg_d[:, c, :] for c in range(DCH)] + [wu_d[:, c, :] for c in range(DCH)]
        ffn_src += [wd_d[:, sum(DOWN_J[:k]) * D:sum(DOWN_J[:k + 1]) * D] for k in range(4)]

        psum = ctx.enter_context(nc.psum_tensor("psum", [P, 4096], FP32))

        def slot(n):
            return psum[:, (n % 4) * 1024:(n % 4 + 1) * 1024]

        def scores_ps(i):
            return psum[:, (i % 2) * HL:(i % 2 + 1) * HL]

        pt_ps = psum[:, 2048:3072]
        out_ps = psum[:, 3072:3584]
        xt_ps = psum[:, 3584:4096]

        def gate_ps(j):
            return psum[:, (j % 2) * 512:(j % 2) * 512 + S]

        def up_ps(j):
            return psum[:, 1024 + (j % 2) * 512:1024 + (j % 2) * 512 + S]

        def x2t_ps(i):
            return psum[:, 2048 + (i % 2) * 512:2048 + (i % 2) * 512 + D]

        def down_ps(i):
            return psum[:, 3072 + (i % 2) * 512:3072 + (i % 2) * 512 + D]

        names = ["g_bound", "g_up", "exp_scale", "v_bound", "v_up", "v_down", "tanh_x", "tanh_f",
                 "attn_gain", "t0", "t1", "h_bound", "h_up", "gate_k", "up_k", "down_k"]

        def s1(name):
            i = names.index(name)
            return sc[:, i:i + 1]

        w_scale = sc[:, 20:23]
        w_inv = sc[:, 23:26]
        w_bound = sc[:, 26:29]
        w_big = sc[:, 29:32]

        ctx_loaded = sem("ctx_loaded")
        wkr_loaded = sem("wkr_loaded")
        keys_loaded = [sem(f"keys_loaded{g}") for g in range(4)]
        wkckv_loaded = sem("wkckv_loaded")
        wq_loaded = [sem(f"wq_loaded{g}") for g in range(4)]
        wo_loaded = [sem(f"wo_loaded{g}") for g in range(4)]
        x_loaded = [sem(f"x_loaded{g}") for g in range(4)]
        params_loaded = sem("params_loaded")
        piece_loaded = [sem(f"piece_loaded{k}") for k in range(2)]
        out_stored = [sem(f"out_stored{k}") for k in range(TPB)]
        ident_zeroed = sem("ident_zeroed")
        ident_ready = sem("ident_ready")
        rope_step = sem("rope_step")
        kv_ready = sem("kv_ready")
        kr_filled = sem("kr_filled")
        kr_copied = sem("kr_copied")
        a1_filled = sem("a1_filled")
        a1_copied = sem("a1_copied")
        t2_filled = sem("t2_filled")
        t2_copied = sem("t2_copied")
        u_filled = sem("u_filled")
        u_copied = sem("u_copied")
        g_filled = sem("g_filled")
        g_hi_ready = sem("g_hi_ready")
        g_lo_ready = sem("g_lo_ready")
        v_filled = sem("v_filled")
        v_hi_ready = sem("v_hi_ready")
        v_lo_ready = sem("v_lo_ready")
        piece_max = sem("piece_max")
        tensor_max = sem("tensor_max")
        max_shared = sem("max_shared")
        sc_step = sem("sc_step")
        g_scales_ready = sem("g_scales_ready")
        v_scales_ready = sem("v_scales_ready")
        ffn_scales_ready = sem("ffn_scales_ready")
        big_ready = sem("big_ready")
        tanh_ready = sem("tanh_ready")
        stats_ready = sem("stats_ready")
        meanvar_ready = sem("meanvar_ready")
        x1_stats_ready = sem("x1_stats_ready")
        x1_meanvar_ready = sem("x1_meanvar_ready")
        ln_step = sem("ln_step")
        ln_ready = sem("ln_ready")
        xn_ready = sem("xn_ready")
        xt_filled = sem("xt_filled")
        xt_hi_ready = sem("xt_hi_ready")
        xt_lo_ready = sem("xt_lo_ready")
        scores_ready = sem("scores_ready")
        row_max_ready = sem("row_max_ready")
        shifted_ready = sem("shifted_ready")
        exp_ready = sem("exp_ready")
        row_sum_ready = sem("row_sum_ready")
        row_inv_ready = sem("row_inv_ready")
        probs_ready = sem("probs_ready")
        pt_filled = sem("pt_filled")
        pt_hi_ready = sem("pt_hi_ready")
        pt_lo_ready = sem("pt_lo_ready")
        attn_ready = sem("attn_ready")
        x1_ready = sem("x1_ready")
        piece_maxed = sem("piece_maxed")
        piece_cast = sem("piece_cast")
        tmp_ready = sem("tmp_ready")
        piece_scaled = sem("piece_scaled")
        piece_split = sem("piece_split")
        xn2_ready = sem("xn2_ready")
        x2t_filled = sem("x2t_filled")
        x2t_hi_ready = sem("x2t_hi_ready")
        x2t_lo_ready = sem("x2t_lo_ready")
        gate_filled = sem("gate_filled")
        up_filled = sem("up_filled")
        silu_ready = sem("silu_ready")
        hidden_ready = sem("hidden_ready")
        h_hi_ready = sem("h_hi_ready")
        h_lo_ready = sem("h_lo_ready")
        down_filled = sem("down_filled")
        down_scaled = sem("down_scaled")
        out_ready = sem("out_ready")

        SLOT_A1, SLOT_T2, SLOT_U, SLOT_G, SLOT_V = 2, 3, 7, 11, 28

        def v_slots(q):
            n = (SLOT_V + 2 * q) % 4
            return psum[:, n * 1024:(n + 2) * 1024]

        def x_tile(t):
            return x_res[:, bass.ds(t, 1), :].rearrange("p a n -> p (a n)")

        block = ctx.enter_context(nc.Block())

        @block.sync
        def _(sp):
            sp.dma_start(ctx_t, ctx_d).then_inc(ctx_loaded, 16)
            sp.dma_start(ctx_s, ctx_swapped_d).then_inc(ctx_loaded, 16)
            sp.dma_start(cos_t, cos_d).then_inc(ctx_loaded, 16)
            sp.dma_start(sin_t, sin_d).then_inc(ctx_loaded, 16)
            sp.dma_start(wkr, wkr_d).then_inc(wkr_loaded, 16)
            for g in range(4):
                sp.dma_start(wqr[:, 4 * g:4 * g + 4], wqr_d[:, 4 * g:4 * g + 4]).then_inc(keys_loaded[g], 16)
                sp.dma_start(wkcq[:, 4 * g:4 * g + 4], wkcq_d[:, 4 * g:4 * g + 4]).then_inc(keys_loaded[g], 16)
            sp.dma_start(wkckv, wkckv_d).then_inc(wkckv_loaded, 16)
            for g in range(4):
                sp.dma_start(wq[:, 4 * g:4 * g + 4], wq_d[:, 4 * g:4 * g + 4]).then_inc(wq_loaded[g], 16)
            for g in range(4):
                sp.dma_start(wo[:, 4 * g:4 * g + 4], wo_d[:, 4 * g:4 * g + 4]).then_inc(wo_loaded[g], 16)
            for g in range(4):
                sp.dma_start(x_res[:, TPB * g:TPB * g + TPB], x_d[:, TPB * g:TPB * g + TPB]).then_inc(x_loaded[g], 16)
            sp.dma_start(gx[:, :], gx_d.partition_broadcast(P)).then_inc(params_loaded, 16)
            sp.dma_start(gf[:, :], gf_d.partition_broadcast(P)).then_inc(params_loaded, 16)
            sp.dma_start(sg[:, :], sg_d).then_inc(params_loaded, 16)
            sp.dma_start(su[:, :], su_d).then_inc(params_loaded, 16)
            sp.dma_start(down_row[:, :], sd_d.partition_broadcast(P)).then_inc(params_loaded, 16)

            sp.wait_ge(scores_ready, 3 * TPB)
            for n in range(PIECES):
                if n >= 2:
                    sp.wait_ge(piece_cast, n - 1)
                    sp.wait_ge(piece_maxed, n - 1)
                sp.dma_start(staged(n), ffn_src[n]).then_inc(piece_loaded[n % 2], 16)
            sp.wait_ge(big_ready, 1)
            again = sp.value_load(big[0:1, 0:1], min_val=0, max_val=1)
            with sp.If(again != 0):
                sp.wait_ge(piece_cast, PIECES)
                sp.wait_ge(piece_maxed, PIECES)
                for n in range(PIECES):
                    if n >= 2:
                        sp.wait_ge(piece_split, n - 1)
                    sp.dma_start(staged(n), ffn_src[n]).then_inc(piece_loaded[n % 2], 16)
            with sp.Fori(0, B) as b:
                for i in range(TPB):
                    sp.wait_ge(out_ready, b * TPB + i + 1)
                    sp.dma_start(out_d[:, bass.ds(b * TPB + i, 1), :], o_sb[i].rearrange("p (a n) -> p a n", a=1)) \
                        .then_inc(out_stored[i], 16)
            for i in range(TPB):
                sp.wait_ge(out_stored[i], 16 * (B + 1))

        @block.gpsimd
        def _(pool):
            nc.gpsimd.memset(ident[:, :], 0.0).then_inc(ident_zeroed, 1)
            pool.wait_ge(ident_zeroed, 1)
            nc.gpsimd.affine_select(out=ident[:, :], in_=ident[:, :], compare_op=ALU.not_equal, fill=1.0,
                                    base=0, pattern=[[-1, P]], channel_multiplier=1).then_inc(ident_ready, 1)
            for k in range(2):
                pool.wait_ge(tensor_max, 2 * k + 2)
                nc.gpsimd.partition_all_reduce(all_max[:, 2 * k:2 * k + 2], tens_max[:, 2 * k:2 * k + 2],
                                               P, RMAX).then_inc(max_shared, 1)
            for n in range(PIECES):
                pool.wait_ge(piece_loaded[n % 2], 16 * (n // 2 + 1))
                nc.gpsimd.tensor_scalar(w_hi(n), staged(n), -ZERO_POINT, 1.0, ALU.add, ALU.mult) \
                    .then_inc(piece_cast, 1)
            pool.wait_ge(tensor_max, 6)
            nc.gpsimd.partition_all_reduce(all_max[:, 4:8], tens_max[:, 4:8], P, RMAX).then_inc(max_shared, 1)
            pool.wait_ge(big_ready, 1)
            again = pool.value_load(big[0:1, 0:1], min_val=0, max_val=1)
            with pool.If(again != 0):
                pool.wait_ge(attn_ready, NT)
                pool.wait_ge(piece_cast, PIECES)
                for n in range(PIECES):
                    w, k = piece_width(n), n // 4
                    pool.wait_ge(piece_loaded[n % 2], 16 * (PIECES // 2 + n // 2 + 1))
                    if n:
                        pool.wait_ge(piece_split, n)
                    nc.gpsimd.tensor_scalar(w_tmp[:, 0:w], staged(n), -ZERO_POINT, w_scale[:, k:k + 1],
                                            ALU.add, ALU.mult).then_inc(tmp_ready, 1)
                    pool.wait_ge(tmp_ready, n + 1)
                    nc.gpsimd.tensor_copy(w_hi(n), w_tmp[:, 0:w]).then_inc(piece_scaled, 1)
                    pool.wait_ge(piece_scaled, n + 1)
                    nc.gpsimd.tensor_tensor(w_lo(n), w_tmp[:, 0:w], w_hi(n), ALU.subtract).then_inc(piece_split, 1)
            with pool.Fori(0, B) as b:
                for i in range(TPB):
                    pool.wait_ge(down_scaled, b * TPB + i + 1)
                    nc.gpsimd.tensor_tensor(o_sb[i], o_sb[i], x_tile(b * TPB + i), ALU.add).then_inc(out_ready, 1)

        @block.scalar
        def _(act):
            for k in range(2):
                act.wait_ge(kr_filled, k + 1)
                nc.scalar.activation(krt[:, 4 * k:4 * k + 4, :].rearrange("p q n -> p (q n)"), slot(k),
                                     ACT.Copy).then_inc(kr_copied, 1)
            for k in range(4):
                act.wait_ge(t2_filled, k + 1)
                nc.scalar.activation(t2[:, k * 1024:(k + 1) * 1024], slot(SLOT_T2 + k), ACT.Copy) \
                    .then_inc(t2_copied, 1)
            for k in range(4):
                act.wait_ge(u_filled, k + 1)
                nc.scalar.activation(u_t[:, k * 1024:(k + 1) * 1024], slot(SLOT_U + k), ACT.Copy) \
                    .then_inc(u_copied, 1)
            act.wait_ge(g_scales_ready, 1)
            for h in range(H):
                act.wait_ge(g_filled, h + 1)
                nc.scalar.activation(g_all[:, 0, :, :, h * L:(h + 1) * L].rearrange("p c b l -> p (c b) l"),
                                     slot(SLOT_G + h).rearrange("p (m l) -> p m l", l=L),
                                     ACT.Copy, scale=s1("g_up")).then_inc(g_hi_ready, 1)
            act.wait_ge(v_scales_ready, 1)
            for q in range(PAIRS):
                act.wait_ge(v_filled, q + 1)
                nc.scalar.activation(v_all[:, q, 0].rearrange("p b n -> p (b n)"), v_slots(q),
                                     ACT.Copy, scale=s1("v_up")).then_inc(v_hi_ready, 1)
                if q == 0:
                    act.wait_ge(params_loaded, 80)
                    nc.scalar.activation(s1("tanh_x"), gx[:, :], ACT.Tanh).then_inc(tanh_ready, 1)
                    nc.scalar.activation(s1("tanh_f"), gf[:, :], ACT.Tanh).then_inc(tanh_ready, 1)

            def normalise(dst, t):
                return nc.scalar.activation(dst, x_tile(t), ACT.Identity, scale=ln_scale[:, bass.ds(t, 1)],
                                            bias=ln_bias[:, bass.ds(t, 1)])

            act.wait_ge(ln_ready, 1)
            for i in range(2):
                normalise(xn[i], i).then_inc(xn_ready, 1)
            act.wait_ge(xt_filled, 1)
            nc.scalar.activation(xt[:, 0, 0].rearrange("p c t -> p (c t)"), xt_ps, ACT.Copy) \
                .then_inc(xt_hi_ready, 1)

            def attention_period(i, k, scores, probs):
                if scores:
                    act.wait_ge(xt_filled, i + 2)
                    nc.scalar.activation(xt[:, (k + 1) % 2, 0].rearrange("p c t -> p (c t)"), xt_ps, ACT.Copy) \
                        .then_inc(xt_hi_ready, 1)
                if probs:
                    act.wait_ge(pt_filled, i)
                    nc.scalar.activation(pt[:, (k + 1) % 2, 0].rearrange("p q t -> p (q t)"), pt_ps, ACT.Copy) \
                        .then_inc(pt_hi_ready, 1)
                if scores:
                    act.wait_ge(shifted_ready, i + 1)
                    nc.scalar.activation(ex[k % 2], ex[k % 2], ACT.Exp, scale=s1("exp_scale")) \
                        .then_inc(exp_ready, 1)
                    normalise(xn[k % 2], (i + 2) % NT).then_inc(xn_ready, 1)

            for k in range(TPB):
                attention_period(k, k, True, k >= 1)
            with act.Fori(1, B) as g:
                for k in range(TPB):
                    attention_period(g * TPB + k, k, True, True)
            attention_period(NT, 0, False, True)

            act.wait_ge(xt_lo_ready, NT + 1)
            act.wait_ge(xn_ready, NT + 2)

            def first_parts_of_x2t(b):
                for i in range(TPB):
                    act.wait_ge(x2t_filled, b * TPB + i + 1)
                    nc.scalar.activation(x2t[:, 0, :, i * P:(i + 1) * P],
                                         x2t_ps(i).rearrange("p (c t) -> p c t", c=DCH), ACT.Copy) \
                        .then_inc(x2t_hi_ready, 1)

            act.wait_ge(ln_ready, 2)
            for i in range(TPB):
                normalise(xn2[i], i).then_inc(xn2_ready, 1)
            first_parts_of_x2t(0)
            act.wait_ge(ffn_scales_ready, 1)
            act.wait_ge(ln_ready, 1 + B)
            with act.Fori(0, B) as b:
                for j in range(JCH):
                    act.wait_ge(gate_filled, b * JCH + j + 1)
                    nc.scalar.activation(sil[j % 2], gate_ps(j), ACT.Silu, scale=sg[:, j:j + 1]) \
                        .then_inc(silu_ready, 1)
                    act.wait_ge(hidden_ready, b * JCH + j + 1)
                    nc.scalar.activation(h_all[:, 0, j, :], hid[j % 2], ACT.Copy).then_inc(h_hi_ready, 1)
                    if j in (1, 3, 5, 7):
                        i = j // 2
                        normalise(xn2[i], (b * TPB + TPB + i) % NT).then_inc(xn2_ready, 1)
                first_parts_of_x2t(b + 1)

        @block.vector
        def _(dve):
            dve.wait_ge(ctx_loaded, 64)

            def by_batch(a):
                return a.rearrange("p (b l) -> p b l", b=B)

            nc.vector.tensor_tensor(by_batch(kvt[:, :]), by_batch(ctx_t),
                                    cos_t.unsqueeze(1).to_broadcast([P, B, L]), ALU.mult).then_inc(rope_step, 1)
            nc.vector.tensor_tensor(by_batch(ctx_s), by_batch(ctx_s),
                                    sin_t.unsqueeze(1).to_broadcast([P, B, L]), ALU.mult).then_inc(rope_step, 1)
            dve.wait_ge(rope_step, 2)
            nc.vector.tensor_tensor(kvt[:, :], kvt[:, :], ctx_s, ALU.add).then_inc(kv_ready, 1)

            dve.wait_ge(a1_filled, 1)
            nc.vector.tensor_copy(a1t.rearrange("p q k -> p (q k)"), slot(SLOT_A1)).then_inc(a1_copied, 1)

            maxed = [0]

            def max_of(src):
                nc.vector.tensor_reduce(part_max[:, maxed[0]:maxed[0] + 1], src, AX.X, ALU.max,
                                        apply_absolute_value=True).then_inc(piece_max, 1)
                maxed[0] += 1

            def max_of_four(k):
                dve.wait_ge(piece_max, maxed[0])
                nc.vector.tensor_reduce(tens_max[:, k:k + 1], part_max[:, 4 * k:4 * k + 4], AX.X, ALU.max) \
                    .then_inc(tensor_max, 1)

            steps = [0]

            def step(instruction):
                instruction.then_inc(sc_step, 1)
                steps[0] += 1
                dve.wait_ge(sc_step, steps[0])

            for k in range(4):
                dve.wait_ge(t2_copied, k + 1)
                max_of(t2[:, k * 1024:(k + 1) * 1024])
            max_of_four(0)
            for g in range(4):
                dve.wait_ge(wq_loaded[g], 16)
                max_of(wq[:, 4 * g:4 * g + 4, :].rearrange("p h n -> p (h n)"))
            max_of_four(1)
            for k in range(4):
                dve.wait_ge(u_copied, k + 1)
                max_of(u_t[:, k * 1024:(k + 1) * 1024])
            max_of_four(2)

            def fold_scales(first, bound, up):
                step(nc.vector.tensor_tensor(s1("t0"), all_max[:, first:first + 1],
                                             all_max[:, first + 1:first + 2], ALU.mult))
                step(nc.vector.tensor_scalar(s1(bound), s1("t0"), float(DK), TINY, ALU.mult, ALU.max))
                step(nc.vector.reciprocal(s1("t1"), s1(bound)))
                step(nc.vector.tensor_scalar(s1(up), s1("t1"), TOP, None, ALU.mult))

            dve.wait_ge(max_shared, 1)
            fold_scales(0, "g_bound", "g_up")
            nc.vector.tensor_scalar(s1("exp_scale"), s1("g_bound"), 1.0 / (TOP * X_SCALE), None, ALU.mult) \
                .then_inc(g_scales_ready, 1)

            for h in range(H):
                dve.wait_ge(g_hi_ready, h + 1)
                nc.vector.scalar_tensor_tensor(
                    out=g_all[:, 1, :, :, h * L:(h + 1) * L].rearrange("p c b l -> p (c b) l"),
                    in0=slot(SLOT_G + h).rearrange("p (m l) -> p m l", l=L), scalar=s1("g_up"),
                    in1=g_all[:, 0, :, :, h * L:(h + 1) * L].rearrange("p c b l -> p (c b) l"),
                    op0=ALU.mult, op1=ALU.subtract).then_inc(g_lo_ready, 1)
                if h in (2, 5, 8, 11):
                    g = h // 3
                    dve.wait_ge(wo_loaded[g], 16)
                    max_of(wo[:, 4 * g:4 * g + 4, :].rearrange("p h n -> p (h n)"))
            max_of_four(3)
            dve.wait_ge(max_shared, 2)
            fold_scales(2, "v_bound", "v_up")
            nc.vector.tensor_scalar(s1("v_down"), s1("v_bound"), 1.0 / (TOP * P_SCALE), None, ALU.mult) \
                .then_inc(v_scales_ready, 1)

            def statistics(i, at):
                return nc.vector.bn_stats(stats[:, at, :], x_tile(i))

            def aggregate(at):
                return nc.vector.bn_aggr(meanvar[:, at, :], stats[:, at, :])

            NEWTONS = 3
            LN_STEPS = 3 + 4 * NEWTONS + 1

            def normalisation(call, first, n):
                v, y, c = (newton[:, m, 0:n] for m in range(3))
                scale, bias = ln_scale[:, bass.ds(first, n)], ln_bias[:, bass.ds(first, n)]
                mean = meanvar[:, 0:n, 0:1].rearrange("p t a -> p (t a)")
                var = meanvar[:, 0:n, 1:2].rearrange("p t a -> p (t a)")
                done = [0]

                def after(instruction):
                    instruction.then_inc(ln_step, 1)
                    done[0] += 1
                    dve.wait_ge(ln_step, call * LN_STEPS + done[0])

                after(nc.vector.tensor_scalar(v, var, EPS, None, ALU.add))
                after(nc.vector.tensor_scalar(y.bitcast(INT32), v.bitcast(INT32), 1, None, ALU.logical_shift_right))
                after(nc.vector.tensor_scalar(y.bitcast(INT32), y.bitcast(INT32), -1.0, float(0x5F3759DF),
                                              ALU.mult, ALU.add))
                for _ in range(NEWTONS):
                    after(nc.vector.tensor_tensor(c, y, y, ALU.mult))
                    after(nc.vector.tensor_tensor(c, c, v, ALU.mult))
                    after(nc.vector.tensor_scalar(c, c, -0.5, 1.5, ALU.mult, ALU.add))
                    after(nc.vector.tensor_tensor(y, y, c, ALU.mult))
                after(nc.vector.tensor_scalar(scale, y, X_SCALE, None, ALU.mult))
                nc.vector.scalar_tensor_tensor(out=bias, in0=mean, scalar=-1.0, in1=scale,
                                               op0=ALU.mult, op1=ALU.mult).then_inc(ln_ready, 1)

            counted = 0
            for q in range(PAIRS):
                dve.wait_ge(v_hi_ready, q + 1)
                nc.vector.scalar_tensor_tensor(
                    out=v_all[:, q, 1].rearrange("p b n -> p (b n)"), in0=v_slots(q), scalar=s1("v_up"),
                    in1=v_all[:, q, 0].rearrange("p b n -> p (b n)"),
                    op0=ALU.mult, op1=ALU.subtract).then_inc(v_lo_ready, 1)
                for t in range(counted, min(counted + 3, NT)):
                    dve.wait_ge(x_loaded[t // TPB], 16)
                    statistics(t, t).then_inc(stats_ready, 1)
                    counted += 1
                    dve.wait_ge(stats_ready, counted)
                    aggregate(t).then_inc(meanvar_ready, 1)
                if q == 5:
                    dve.wait_ge(meanvar_ready, NT)
                    normalisation(0, 0, NT)
            dve.wait_ge(tanh_ready, 2)
            step(nc.vector.tensor_tensor(s1("attn_gain"), s1("tanh_x"), s1("v_down"), ALU.mult))

            def hold():
                dve.wait_ge(tanh_ready, 2)

            def by_head(a):
                return a.rearrange("p (h l) -> p h l", h=H)

            def attention_period(i, k, scores, probs, attn):
                m = k % 2
                if scores:
                    dve.wait_ge(scores_ready, i + 1)
                    nc.vector.tensor_reduce(row_max[:, m, :], by_head(scores_ps(k)), AX.X, ALU.max) \
                        .then_inc(row_max_ready, 1)
                    dve.wait_ge(row_max_ready, i + 1)
                    nc.vector.tensor_tensor(by_head(ex[m]), by_head(scores_ps(k)),
                                            row_max[:, m, :].unsqueeze(2).to_broadcast([P, H, L]),
                                            ALU.subtract).then_inc(shifted_ready, 1)
                    dve.wait_ge(xt_hi_ready, i + 2)
                    nc.vector.tensor_tensor(xt[:, (k + 1) % 2, 1].rearrange("p c t -> p (c t)"), xt_ps,
                                            xt[:, (k + 1) % 2, 0].rearrange("p c t -> p (c t)"),
                                            ALU.subtract).then_inc(xt_lo_ready, 1)
                if probs:
                    dve.wait_ge(pt_hi_ready, i)
                    nc.vector.tensor_tensor(pt[:, (k + 1) % 2, 1].rearrange("p q t -> p (q t)"), pt_ps,
                                            pt[:, (k + 1) % 2, 0].rearrange("p q t -> p (q t)"),
                                            ALU.subtract).then_inc(pt_lo_ready, 1)
                if scores:
                    dve.wait_ge(exp_ready, i + 1)
                    nc.vector.tensor_reduce(row_sum[:, m, :], by_head(ex[m]), AX.X, ALU.add) \
                        .then_inc(row_sum_ready, 1)
                    dve.wait_ge(row_sum_ready, i + 1)
                    nc.vector.reciprocal(row_inv[:, m, :], row_sum[:, m, :]).then_inc(row_inv_ready, 1)
                    dve.wait_ge(row_inv_ready, i + 1)
                    nc.vector.scalar_tensor_tensor(out=by_head(ex[m]), in0=by_head(ex[m]), scalar=P_SCALE,
                                                   in1=row_inv[:, m, :].unsqueeze(2).to_broadcast([P, H, L]),
                                                   op0=ALU.mult, op1=ALU.mult).then_inc(probs_ready, 1)
                if attn:
                    dve.wait_ge(attn_ready, i - 1)
                    nc.vector.scalar_tensor_tensor(out=x_tile(i - 2), in0=out_ps, scalar=s1("attn_gain"),
                                                   in1=x_tile(i - 2), op0=ALU.mult, op1=ALU.add) \
                        .then_inc(x1_ready, 1)
                    hold()
                    dve.wait_ge(x1_ready, i - 1)
                    statistics(i - 2, (k + 2) % TPB).then_inc(x1_stats_ready, 1)
                    hold()
                    dve.wait_ge(x1_stats_ready, i - 1)
                    aggregate((k + 2) % TPB).then_inc(x1_meanvar_ready, 1)

            def batch_normalisation(g):
                dve.wait_ge(x1_meanvar_ready, g * TPB)
                normalisation(g, (g - 1) * TPB, TPB)

            def maxima_of_pieces(n0, n1):
                for n in range(n0, n1):
                    dve.wait_ge(piece_loaded[n % 2], 16 * (n // 2 + 1))
                    nc.vector.tensor_reduce(ffn_max[:, n:n + 1], staged(n), AX.X, ALU.max,
                                            apply_absolute_value=True).then_inc(piece_maxed, 1)

            dve.wait_ge(xt_hi_ready, 1)
            nc.vector.tensor_tensor(xt[:, 0, 1].rearrange("p c t -> p (c t)"), xt_ps,
                                    xt[:, 0, 0].rearrange("p c t -> p (c t)"), ALU.subtract) \
                .then_inc(xt_lo_ready, 1)
            for k in range(TPB):
                attention_period(k, k, True, k >= 1, k >= 2)
            with dve.Fori(1, B - 1) as g:
                for k in range(TPB):
                    attention_period(g * TPB + k, k, True, True, True)
                    if k == 1:
                        batch_normalisation(g)
            for k in range(TPB + 2):
                i = (B - 1) * TPB + k
                attention_period(i, k, k < TPB, k <= TPB, True)
                if k % TPB == 1:
                    batch_normalisation(i // TPB)
                maxima_of_pieces(2 * k, 2 * k + 2)

            step(nc.vector.tensor_tensor(sgsu[:, :], sg[:, :], su[:, :], ALU.mult))
            nc.vector.tensor_reduce(tens_max[:, 7:8], sgsu[:, :], AX.X, ALU.max,
                                    apply_absolute_value=True).then_inc(tensor_max, 1)
            dve.wait_ge(piece_maxed, PIECES)
            nc.vector.tensor_reduce(tens_max[:, 4:7], ffn_max[:, :].rearrange("p (m n) -> p m n", m=3),
                                    AX.X, ALU.max).then_inc(tensor_max, 1)
            dve.wait_ge(max_shared, 3)
            step(nc.vector.tensor_scalar(w_big, all_max[:, 4:7], EXACT - ZERO_POINT, None, ALU.is_gt))
            step(nc.vector.tensor_reduce(s1("t0"), w_big, AX.X, ALU.max))
            nc.vector.tensor_copy(big[:, :], s1("t0")).then_inc(big_ready, 1)
            step(nc.vector.tensor_scalar(w_bound, all_max[:, 4:7], ZERO_POINT, None, ALU.add))
            step(nc.vector.reciprocal(w_scale, w_bound))
            step(nc.vector.tensor_scalar(w_scale, w_scale, EXACT, 1.0, ALU.mult, ALU.subtract))
            step(nc.vector.tensor_tensor(w_scale, w_scale, w_big, ALU.mult))
            step(nc.vector.tensor_scalar(w_scale, w_scale, 1.0, None, ALU.add))
            step(nc.vector.reciprocal(w_inv, w_scale))
            step(nc.vector.tensor_tensor(s1("t0"), w_bound[:, 0:1], w_bound[:, 1:2], ALU.mult))
            step(nc.vector.tensor_tensor(s1("t0"), s1("t0"), all_max[:, 7:8], ALU.mult))
            step(nc.vector.tensor_scalar(s1("h_bound"), s1("t0"), float(D) * D, TINY, ALU.mult, ALU.max))
            step(nc.vector.reciprocal(s1("t1"), s1("h_bound")))
            step(nc.vector.tensor_scalar(s1("gate_k"), w_inv[:, 0:1], 1.0 / X_SCALE, None, ALU.mult))
            step(nc.vector.tensor_scalar(s1("up_k"), w_inv[:, 1:2], s1("t1"), TOP / X_SCALE, ALU.mult, ALU.mult))
            step(nc.vector.tensor_scalar(s1("down_k"), w_inv[:, 2:3], s1("h_bound"), 1.0 / TOP, ALU.mult, ALU.mult))
            step(nc.vector.tensor_tensor(s1("down_k"), s1("down_k"), s1("tanh_f"), ALU.mult))
            step(nc.vector.tensor_scalar(sg[:, :], sg[:, :], s1("gate_k"), None, ALU.mult))
            step(nc.vector.tensor_scalar(su[:, :], su[:, :], s1("up_k"), None, ALU.mult))
            nc.vector.tensor_scalar(down_row[:, :], down_row[:, :], s1("down_k"), None, ALU.mult) \
                .then_inc(ffn_scales_ready, 1)

            def second_parts_of_x2t(b):
                for i in range(TPB):
                    dve.wait_ge(x2t_hi_ready, b * TPB + i + 1)
                    nc.vector.tensor_tensor(x2t[:, 1, :, i * P:(i + 1) * P],
                                            x2t_ps(i).rearrange("p (c t) -> p c t", c=DCH),
                                            x2t[:, 0, :, i * P:(i + 1) * P], ALU.subtract) \
                        .then_inc(x2t_lo_ready, 1)

            for i in range(TPB):
                dve.sem_inc(out_stored[i], 16)
            second_parts_of_x2t(0)
            dve.wait_ge(ffn_scales_ready, 1)
            with dve.Fori(0, B) as b:
                for j in range(JCH):
                    dve.wait_ge(up_filled, b * JCH + j + 1)
                    dve.wait_ge(silu_ready, b * JCH + j + 1)
                    nc.vector.scalar_tensor_tensor(out=hid[j % 2], in0=up_ps(j), scalar=su[:, j:j + 1],
                                                   in1=sil[j % 2], op0=ALU.mult, op1=ALU.mult) \
                        .then_inc(hidden_ready, 1)
                    dve.wait_ge(h_hi_ready, b * JCH + j + 1)
                    nc.vector.tensor_tensor(h_all[:, 1, j, :], hid[j % 2], h_all[:, 0, j, :], ALU.subtract) \
                        .then_inc(h_lo_ready, 1)
                second_parts_of_x2t(b + 1)
                for i in range(TPB):
                    dve.wait_ge(down_filled, b * TPB + i + 1)
                    dve.wait_ge(out_stored[i], 16 * (b + 1))
                    nc.vector.tensor_tensor(o_sb[i], down_ps(i), down_row[:, :], ALU.mult).then_inc(down_scaled, 1)

        @block.tensor
        def _(pe):
            pe.wait_ge(wkr_loaded, 16)
            pe.wait_ge(kv_ready, 1)
            for q in range(PAIRS):
                last = nc.tensor.matmul(psum[:, q * BL:(q + 1) * BL], wkr[:, q * P:(q + 1) * P], kvt[:, :],
                                        start=True, stop=True)
                if q % 4 == 3:
                    last.then_inc(kr_filled, 1)
            for q in range(PAIRS):
                if q % 2 == 0:
                    pe.wait_ge(keys_loaded[q // 2], 32)
                for c in range(QCH):
                    for h in (2 * q, 2 * q + 1):
                        half = (h % 2) * R
                        last = nc.tensor.matmul(slot(SLOT_A1)[half:half + R, q * DK:(q + 1) * DK],
                                                wqr[:, h, c, :], wkcq[:, h, c, :],
                                                start=c == 0, stop=c == QCH - 1)
            last.then_inc(a1_filled, 1)
            pe.wait_ge(kr_copied, 2)
            pe.wait_ge(a1_copied, 1)
            for h in range(H):
                half = (h % 2) * R
                at_h = (t2_at(h) % 4) * BL
                last = nc.tensor.matmul(slot(SLOT_T2 + h // 4)[:, at_h:at_h + BL], a1t[half:half + R, h // 2, :],
                                        krt[half:half + R, h // 2, :], start=True, stop=True)
                if h % 4 == 3:
                    last.then_inc(t2_filled, 1)
            pe.wait_ge(wkckv_loaded, 16)
            for h in range(H):
                if h % 4 == 0:
                    pe.wait_ge(t2_copied, h // 4 + 1)
                last = nc.tensor.matmul(slot(SLOT_U + h // 4)[:, (h % 4) * BL:(h % 4 + 1) * BL],
                                        wkckv[:, h * DK:(h + 1) * DK], kvt[:, :], start=True, stop=True)
                if h % 4 == 3:
                    last.then_inc(u_filled, 1)
            pe.wait_ge(t2_copied, 4)
            for h in range(H):
                if h % 4 == 0:
                    pe.wait_ge(wq_loaded[h // 4], 16)
                if h < 4:
                    pe.wait_ge(u_copied, h + 1)
                else:
                    pe.wait_ge(g_lo_ready, h - 3)
                for c in range(DCH):
                    last = nc.tensor.matmul(slot(SLOT_G + h)[:, c * BL:(c + 1) * BL], wq[:, h, c * P:(c + 1) * P],
                                            t2[:, t2_at(h) * BL:(t2_at(h) + 1) * BL], start=True, stop=True)
                last.then_inc(g_filled, 1)
            pe.wait_ge(u_copied, 4)
            for q in range(PAIRS):
                if q % 2 == 0:
                    pe.wait_ge(wo_loaded[q // 2], 16)
                if q < 2:
                    pe.wait_ge(g_lo_ready, H - 1 + q)
                else:
                    pe.wait_ge(v_lo_ready, q - 1)
                for b in range(B):
                    for h in (2 * q, 2 * q + 1):
                        half = (h % 2) * L
                        at_u = h * BL + b * L
                        last = nc.tensor.matmul(v_slots(q)[half:half + L, b * D:(b + 1) * D],
                                                u_t[:, at_u:at_u + L], wo[:, h, :], start=True, stop=True)
                last.then_inc(v_filled, 1)

            def transpose_rows(dst, src):
                for c in range(DCH):
                    last = nc.tensor.transpose(dst[:, c * P:(c + 1) * P], src[:, c * P:(c + 1) * P], ident[:, :])
                return last

            def g_at(s, c, b, n):
                return g_region[:, bass.ds((s * DCH + c) * B * HL + b * HL + n * 512, 512)]

            def v_at(q, s, b):
                return v_region[:, bass.ds((q * 2 + s) * B * D + b * D, D)]

            def attention_period(i, k, b, scores, probs, attn):
                if scores:
                    pe.wait_ge(xt_lo_ready, i + 1)
                    if not isinstance(i, int) or i >= 2:
                        pe.wait_ge(shifted_ready, i - 1)
                    m = k % 2
                    for c in range(DCH):
                        for sx, sy in ((0, 0), (0, 1), (1, 0)):
                            for n in range(HL // 512):
                                last = nc.tensor.matmul(scores_ps(k)[:, n * 512:(n + 1) * 512], xt[:, m, sx, c, :],
                                                        g_at(sy, c, b, n), start=c == 0 and sx + sy == 0,
                                                        stop=c == DCH - 1 and sx == 1)
                    last.then_inc(scores_ready, 1)
                    pe.wait_ge(xn_ready, i + 2)
                    transpose_rows(xt_ps, xn[(k + 1) % 2]).then_inc(xt_filled, 1)
                if probs:
                    pe.wait_ge(probs_ready, i)
                    if not isinstance(i, int) or i >= 2:
                        pe.wait_ge(pt_lo_ready, i - 1)
                    for q in range(PAIRS):
                        last = nc.tensor.transpose(pt_ps[:, q * P:(q + 1) * P],
                                                   ex[(k + 1) % 2][:, q * P:(q + 1) * P], ident[:, :])
                    last.then_inc(pt_filled, 1)
                if attn:
                    pe.wait_ge(pt_lo_ready, i - 1)
                    if not isinstance(i, int) or i >= 3:
                        pe.wait_ge(x1_ready, i - 2)
                    bb = b if k % TPB >= 2 else b - 1
                    for q in range(PAIRS):
                        for sx, sy in ((0, 0), (0, 1), (1, 0)):
                            last = nc.tensor.matmul(out_ps, pt[:, k % 2, sx, q, :], v_at(q, sy, bb),
                                                    start=q == 0 and sx + sy == 0,
                                                    stop=q == PAIRS - 1 and sx == 1)
                    last.then_inc(attn_ready, 1)

            pe.wait_ge(ident_ready, 1)
            pe.wait_ge(v_lo_ready, PAIRS)
            pe.wait_ge(xn_ready, 1)
            transpose_rows(xt_ps, xn[0]).then_inc(xt_filled, 1)
            for k in range(TPB):
                attention_period(k, k, 0, True, k >= 1, k >= 2)
            with pe.Fori(1, B) as g:
                for k in range(TPB):
                    attention_period(g * TPB + k, k, g, True, True, True)
            attention_period(NT, 0, B, False, True, True)
            attention_period(NT + 1, 1, B, False, False, True)

            def transpose_batch(b):
                for i in range(TPB):
                    pe.wait_ge(xn2_ready, b * TPB + i + 1)
                    if not isinstance(b, int):
                        pe.wait_ge(x2t_lo_ready, b * TPB + max(i - 1, 0))
                    elif i >= 2:
                        pe.wait_ge(x2t_lo_ready, i - 1)
                    transpose_rows(x2t_ps(i), xn2[i]).then_inc(x2t_filled, 1)

            def feed_forward(parts):
                with pe.Fori(0, B) as b:
                    pe.wait_ge(x2t_lo_ready, b * TPB + TPB)
                    for j in range(JCH):
                        for first, ps, filled, freed in ((0, gate_ps(j), gate_filled, silu_ready),
                                                         (DCH, up_ps(j), up_filled, hidden_ready)):
                            if j >= 2:
                                pe.wait_ge(freed, b * JCH + j - 1)
                            for c in range(DCH):
                                for sx, w in parts:
                                    last = nc.tensor.matmul(ps, w(first + c)[:, j * P:(j + 1) * P], x2t[:, sx, c, :],
                                                            start=c == 0 and (sx, w) == parts[0],
                                                            stop=c == DCH - 1 and (sx, w) == parts[-1])
                            last.then_inc(filled, 1)
                    transpose_batch(b + 1)
                    pe.wait_ge(h_lo_ready, b * JCH + JCH)
                    for i in range(TPB):
                        if i >= 2:
                            pe.wait_ge(down_scaled, b * TPB + i - 1)
                        for j in range(JCH):
                            n, m = down_piece(j)
                            for sx, w in parts:
                                last = nc.tensor.matmul(down_ps(i), h_all[:, sx, j, i * P:(i + 1) * P],
                                                        w(8 + n)[:, m * D:(m + 1) * D],
                                                        start=j == 0 and (sx, w) == parts[0],
                                                        stop=j == JCH - 1 and (sx, w) == parts[-1])
                        last.then_inc(down_filled, 1)

            pe.wait_ge(pt_lo_ready, NT)
            transpose_batch(0)
            pe.wait_ge(shifted_ready, NT)
            pe.wait_ge(x1_ready, NT)
            pe.wait_ge(xt_lo_ready, NT + 1)
            pe.wait_ge(piece_cast, PIECES)
            pe.wait_ge(big_ready, 1)
            general = pe.value_load(big[0:1, 0:1], min_val=0, max_val=1)
            with pe.If(general != 0):
                pe.wait_ge(piece_split, PIECES)
                feed_forward([(0, w_hi), (0, w_lo), (1, w_hi)])
            with pe.Else():
                feed_forward([(0, w_hi), (1, w_hi)])


def kernel(x, ctx_512, g_xattn, g_ffn, L0_xattn_Wq, L0_xattn_w_kc_q, L0_xattn_w_kc_kv, L0_xattn_W_qr,
           L0_xattn_W_kr, L0_xattn_Wo, L0_ffn_wq_gate, L0_ffn_s_gate, L0_ffn_wq_up, L0_ffn_s_up,
           L0_ffn_wq_down, L0_ffn_s_down):
    import numpy as np
    import concourse.bacc as bacc
    from concourse.bass_utils import run_bass_kernel_spmd

    inv_freq = (1.0 / np.float32(10000.0) ** (np.arange(0, DC, 2, dtype=np.float32) / np.float32(DC)))
    freqs = np.arange(L, dtype=np.float32)[:, None] * inv_freq.astype(np.float32)[None, :]
    cos = np.repeat(np.cos(freqs), 2, axis=-1).T
    sin = np.repeat(np.sin(freqs), 2, axis=-1).T
    sign = np.where(np.arange(DC) < DC // 2, -1.0, 1.0).astype(np.float32)[:, None]

    a = {k: np.asarray(v) for k, v in dict(
        x=x, ctx=ctx_512, gx=g_xattn, gf=g_ffn, wq=L0_xattn_Wq, wkcq=L0_xattn_w_kc_q, wkckv=L0_xattn_w_kc_kv,
        wqr=L0_xattn_W_qr, wkr=L0_xattn_W_kr, wo=L0_xattn_Wo, wg=L0_ffn_wq_gate, wu=L0_ffn_wq_up,
        wd=L0_ffn_wq_down, sg=L0_ffn_s_gate, su=L0_ffn_s_up, sd=L0_ffn_s_down).items()}
    ctx_t = a["ctx"].reshape(BL, DC).T
    laid = [
        ("x", a["x"].reshape(NT, P, D).transpose(1, 0, 2)),
        ("ctx_t", ctx_t),
        ("ctx_swapped", np.concatenate([ctx_t[DC // 2:], ctx_t[:DC // 2]])),
        ("cos", cos.astype(np.float32)),
        ("sin", (sin * sign).astype(np.float32)),
        ("gx", a["gx"]),
        ("gf", a["gf"]),
        ("wq", a["wq"].reshape(H, DK, D).transpose(1, 0, 2)),
        ("wkcq", a["wkcq"].reshape(H, DK, QCH, P).transpose(3, 0, 2, 1)),
        ("wkckv", a["wkckv"].transpose(2, 0, 1).reshape(DC, H * DK)),
        ("wqr", a["wqr"].reshape(H, QCH, P, R).transpose(2, 0, 1, 3)),
        ("wkr", a["wkr"].transpose(1, 0, 2).reshape(DC, H * R)),
        ("wo", a["wo"].T.reshape(H, DK, D).transpose(1, 0, 2)),
        ("wg", a["wg"].T.reshape(DCH, P, HID).transpose(1, 0, 2)),
        ("wu", a["wu"].T.reshape(DCH, P, HID).transpose(1, 0, 2)),
        ("wd", a["wd"].T.reshape(JCH, P, D).transpose(1, 0, 2).reshape(P, JCH * D)),
        ("sg", a["sg"].reshape(JCH, P).T),
        ("su", a["su"].reshape(JCH, P).T),
        ("sd", a["sd"]),
    ]
    nc = bacc.Bacc("TRN2", target_bir_lowering=False, num_devices=1)
    arrays, aps = {}, []
    for name, v in laid:
        v = np.ascontiguousarray(v)
        arrays[f"in_{name}"] = v
        aps.append(nc.dram_tensor(f"in_{name}", v.shape, mybir.dt.from_np(v.dtype), kind="ExternalInput").ap())
    aps.append(nc.dram_tensor("out_0", (P, NT, D), FP32, kind="ExternalOutput").ap())
    gated_block(nc, *aps)
    r = run_bass_kernel_spmd(nc, [arrays], core_ids=[0])
    out = r.results[0]["out_0"]
    return np.ascontiguousarray(np.asarray(out).transpose(1, 0, 2)).reshape(B, S, D)
```

```python
import concourse.bass as bass
from concourse import mybir
from contextlib import ExitStack

FP32 = mybir.dt.float32
FP16 = mybir.dt.float16
INT32 = mybir.dt.int32
ALU = mybir.AluOpType
ACT = mybir.ActivationFunctionType
AX = mybir.AxisListType
RMAX = bass.bass_isa.ReduceOp.max

P = 128
B, S, D = 4, 512, 512
H, L = 16, 64
DK = 128
DC = 128
CQ = 384
R = 64
HID = 1408
DCH = D // P
QCH = CQ // P
JCH = HID // P
TPB = S // P
NT = B * TPB
PAIRS = H // 2
BL = B * L
HL = H * L
EPS = 1e-5
ZERO_POINT = 128.0

X_SCALE = 256.0
P_SCALE = 4096.0
TOP = 32768.0
EXACT = 2048.0
TINY = 1e-30

DOWN_J = (3, 3, 3, 2)
PIECES = 3 * 4
HOLE = 3 * 1024


def down_piece(j):
    return j // DOWN_J[0], j % DOWN_J[0]


def piece_width(n):
    return HID if n < 8 else DOWN_J[n - 8] * D


def t2_at(h):
    return (h // 4) * 4 + (h % 2) * 2 + (h // 2) % 2


def gated_block(nc, x_d, ctx_d, ctx_swapped_d, cos_d, sin_d, gx_d, gf_d, wq_d, wkcq_d, wkckv_d,
                wqr_d, wkr_d, wo_d, wg_d, wu_d, wd_d, sg_d, su_d, sd_d, out_d):
    ctx = ExitStack()
    with ctx:
        def sb(name, shape, dt):
            return ctx.enter_context(nc.sbuf_tensor(name, shape, dt))

        def sem(name):
            return ctx.enter_context(nc.semaphore(name))

        g_region = sb("g_region", [P, 2 * DCH * B * HL], FP16)
        v_region = sb("v_region", [P, PAIRS * 2 * B * D], FP16)
        x_res = sb("x_res", [P, NT, D], FP32)
        work = sb("work", [P, 8192], FP32)
        ident = sb("ident", [P, P], FP32)
        kvt = sb("kvt", [P, BL], FP32)
        down_row = sb("down_row", [P, D], FP32)
        sg = sb("sg", [P, JCH], FP32)
        su = sb("su", [P, JCH], FP32)
        sgsu = sb("sgsu", [P, JCH], FP32)
        gx = sb("gx", [P, 1], FP32)
        gf = sb("gf", [P, 1], FP32)
        x_stats = sb("x_stats", [P, TPB, 6], FP32)
        x_meanvar = sb("x_meanvar", [P, TPB, 2], FP32)
        stats = sb("stats", [P, TPB, 6], FP32)
        meanvar = sb("meanvar", [P, TPB, 2], FP32)
        ln_scale = sb("ln_scale", [P, NT], FP32)
        ln_bias = sb("ln_bias", [P, NT], FP32)
        newton = sb("newton", [P, 3, TPB], FP32)
        spare = sb("spare", [P, TPB * D], FP32)
        row_max = sb("row_max", [P, 2, H], FP32)
        row_sum = sb("row_sum", [P, 2, H], FP32)
        row_inv = sb("row_inv", [P, 2, H], FP32)
        part_max = sb("part_max", [P, 20], FP32)
        tens_max = sb("tens_max", [P, 8], FP32)
        all_max = sb("all_max", [P, 8], FP32)
        ffn_max = sb("ffn_max", [P, PIECES], FP32)
        part_sum = sb("part_sum", [P, 8], FP32)
        sc = sb("sc", [P, 32], FP32)
        big = sb("big", [P, 1], INT32)

        g_all = g_region[:, :].rearrange("p (s c b n) -> p s c b n", s=2, c=DCH, b=B)
        v_all = v_region[:, :].rearrange("p (q s b n) -> p q s b n", q=PAIRS, s=2, b=B)
        g32 = g_region[:, :].bitcast(FP32)
        at = 0
        wkcq = g32[:, at:at + H * QCH * DK].rearrange("p (h c k) -> p h c k", h=H, c=QCH)
        at += H * QCH * DK
        wqr = g32[:, at:at + H * QCH * R].rearrange("p (h c r) -> p h c r", h=H, c=QCH)
        at += H * QCH * R
        wkr = g32[:, at:at + H * R]
        at += H * R
        wkckv = g32[:, at:at + H * DK]
        at += H * DK
        ctx_t = g32[:, at:at + BL]
        ctx_s = g32[:, at + BL:at + 2 * BL]
        cos_t = g32[:, at + 2 * BL:at + 2 * BL + L]
        sin_t = g32[:, at + 2 * BL + L:at + 2 * BL + 2 * L]
        at_end = at + 2 * BL + 2 * L
        v32 = v_region[:, :].bitcast(FP32)
        wq = x_res
        wo = v32[:, H * D:2 * H * D].rearrange("p (h n) -> p h n", h=H)

        t2 = work[:, 0:H * BL]
        ex = [work[:, i * HL:(i + 1) * HL] for i in range(2)]
        x2t = work[:, 2048:4096].bitcast(FP16).rearrange("p (s c t) -> p s c t", s=2, c=DCH)
        u_t = work[:, 4096:8192]
        a1t = work[:, 4096:4096 + PAIRS * DK].rearrange("p (q k) -> p q k", q=PAIRS)
        pt = work[:, 4096:6144].bitcast(FP16).rearrange("p (i s q t) -> p i s q t", i=2, s=2, q=PAIRS)
        xn = [work[:, 6144 + i * D:6144 + (i + 1) * D] for i in range(2)]
        xt = work[:, 7168:8192].bitcast(FP16).rearrange("p (i s c t) -> p i s c t", i=2, s=2, c=DCH)
        sil = [work[:, 4096 + i * S:4096 + (i + 1) * S] for i in range(2)]
        hid = [work[:, 5120 + i * S:5120 + (i + 1) * S] for i in range(2)]
        o_sb = [work[:, 6144 + i * D:6144 + (i + 1) * D] for i in range(TPB)]
        junk = g_region[:, 2 * at_end:2 * at_end + 4 * D]
        krt = spare[:, :].rearrange("p (q n) -> p q n", q=PAIRS)
        xn2 = [spare[:, i * D:(i + 1) * D] for i in range(TPB)]

        def hole(k):
            return g_region[:, k * B * HL:k * B * HL + HOLE]

        def w_hi(n):
            w = piece_width(n)
            return hole(n // 2)[:, (n % 2) * (HOLE // 2):(n % 2) * (HOLE // 2) + w]

        def staged(n):
            room = (work[:, 2048:4096], hole(6), hole(7))[n % 3]
            return room.bitcast(INT32)[:, 0:piece_width(n)]

        def staged_again(n):
            return hole(6 + n % 2).bitcast(INT32)[:, 0:piece_width(n)]

        def w_lo(n):
            return v_region[:, n * (HOLE // 2):n * (HOLE // 2) + piece_width(n)]

        widest = HOLE // 2
        h_all = v_region[:, PIECES * widest:PIECES * widest + 2 * JCH * S] \
            .rearrange("p (s j t) -> p s j t", s=2, j=JCH)
        w_tmp = v_region[:, PIECES * widest + 2 * JCH * S:PIECES * widest + 2 * JCH * S + 2 * widest].bitcast(FP32)

        ffn_src = [wg_d[:, c, :] for c in range(DCH)] + [wu_d[:, c, :] for c in range(DCH)]
        ffn_src += [wd_d[:, sum(DOWN_J[:k]) * D:sum(DOWN_J[:k + 1]) * D] for k in range(4)]

        psum = ctx.enter_context(nc.psum_tensor("psum", [P, 4096], FP32))

        def slot(n):
            return psum[:, (n % 4) * 1024:(n % 4 + 1) * 1024]

        def scores_ps(i):
            return psum[:, (i % 2) * HL:(i % 2 + 1) * HL]

        pt_ps = psum[:, 2048:3072]
        out_ps = psum[:, 3072:3584]
        xt_ps = psum[:, 3584:4096]

        def gate_ps(j):
            return psum[:, (j % 2) * 512:(j % 2) * 512 + S]

        def up_ps(j):
            return psum[:, 1024 + (j % 2) * 512:1024 + (j % 2) * 512 + S]

        def bank(i):
            return psum[:, i * 512:(i + 1) * 512]

        def x2t_ps(i):
            return bank((4, 5, (JCH - 2) % 2, 2 + (JCH - 2) % 2)[i])

        def down_ps(i):
            return psum[:, 3072 + (i % 2) * 512:3072 + (i % 2) * 512 + D]

        names = ["g_up", "exp_scale", "v_up", "v_down", "tanh_x", "tanh_f",
                 "attn_gain", "t0", "t1", "h_bound", "h_up", "gate_k", "up_k", "down_k"]

        def s1(name):
            i = names.index(name)
            return sc[:, i:i + 1]

        w_scale = sc[:, 20:23]
        w_inv = sc[:, 23:26]
        w_bound = sc[:, 26:29]
        w_big = sc[:, 29:32]

        ctx_loaded = sem("ctx_loaded")
        wkr_loaded = sem("wkr_loaded")
        keys_loaded = [sem(f"keys_loaded{g}") for g in range(4)]
        wkckv_loaded = sem("wkckv_loaded")
        wq_loaded = [sem(f"wq_loaded{g}") for g in range(4)]
        wo_loaded = [sem(f"wo_loaded{g}") for g in range(4)]
        x_loaded = [sem(f"x_loaded{g}") for g in range(4)]
        params_loaded = sem("params_loaded")
        piece_loaded = [sem(f"piece_loaded{k}") for k in range(3)]
        out_stored = [sem(f"out_stored{k}") for k in range(TPB)]
        ident_zeroed = sem("ident_zeroed")
        ident_ready = sem("ident_ready")
        rope_step = sem("rope_step")
        kv_ready = sem("kv_ready")
        kr_filled = sem("kr_filled")
        kr_copied = sem("kr_copied")
        a1_filled = sem("a1_filled")
        a1_copied = sem("a1_copied")
        t2_filled = sem("t2_filled")
        t2_copied = sem("t2_copied")
        u_filled = sem("u_filled")
        u_copied = sem("u_copied")
        g_filled = sem("g_filled")
        g_hi_ready = sem("g_hi_ready")
        g_lo_ready = sem("g_lo_ready")
        v_filled = sem("v_filled")
        v_hi_ready = sem("v_hi_ready")
        v_lo_ready = sem("v_lo_ready")
        piece_max = sem("piece_max")
        squares_ready = sem("squares_ready")
        tensor_max = sem("tensor_max")
        max_shared = sem("max_shared")
        sc_step = sem("sc_step")
        g_scales_ready = sem("g_scales_ready")
        v_scales_ready = sem("v_scales_ready")
        ffn_scales_ready = sem("ffn_scales_ready")
        big_ready = sem("big_ready")
        tanh_ready = sem("tanh_ready")
        stats_ready = sem("stats_ready")
        meanvar_ready = sem("meanvar_ready")
        x1_stats_ready = sem("x1_stats_ready")
        x1_meanvar_ready = sem("x1_meanvar_ready")
        ln_step = sem("ln_step")
        ln_ready = sem("ln_ready")
        xn_ready = sem("xn_ready")
        xt_filled = sem("xt_filled")
        xt_hi_ready = sem("xt_hi_ready")
        xt_lo_ready = sem("xt_lo_ready")
        scores_ready = sem("scores_ready")
        row_max_ready = sem("row_max_ready")
        shifted_ready = sem("shifted_ready")
        exp_ready = sem("exp_ready")
        row_sum_ready = sem("row_sum_ready")
        row_inv_ready = sem("row_inv_ready")
        probs_ready = sem("probs_ready")
        pt_filled = sem("pt_filled")
        pt_hi_ready = sem("pt_hi_ready")
        pt_lo_ready = sem("pt_lo_ready")
        attn_ready = sem("attn_ready")
        x1_ready = sem("x1_ready")
        piece_maxed = sem("piece_maxed")
        piece_cast = sem("piece_cast")
        tmp_ready = sem("tmp_ready")
        piece_scaled = sem("piece_scaled")
        piece_split = sem("piece_split")
        xn2_ready = sem("xn2_ready")
        x2t_filled = sem("x2t_filled")
        x2t_hi_ready = sem("x2t_hi_ready")
        x2t_lo_ready = sem("x2t_lo_ready")
        gate_filled = sem("gate_filled")
        up_filled = sem("up_filled")
        silu_ready = sem("silu_ready")
        hidden_ready = sem("hidden_ready")
        h_hi_ready = sem("h_hi_ready")
        h_lo_ready = sem("h_lo_ready")
        down_filled = sem("down_filled")
        down_scaled = sem("down_scaled")
        out_ready = sem("out_ready")

        SLOT_U = PAIRS // 4
        SLOT_V = SLOT_U + H // 4
        SLOT_A1 = SLOT_V + 2 * PAIRS
        SLOT_T2 = SLOT_A1 + 1
        SLOT_G = SLOT_T2 + H // 4

        def v_part(s, v):
            return v_all[:, v // 2, s, v % 2 * 2:v % 2 * 2 + 2].rearrange("p b n -> p (b n)")

        def by_head(a):
            return a.rearrange("p (h l) -> p h l", h=H)

        def x_tile(t):
            return x_res[:, bass.ds(t, 1), :].rearrange("p a n -> p (a n)")

        block = ctx.enter_context(nc.Block())

        @block.sync
        def _(sp):
            sp.dma_start(ctx_t, ctx_d).then_inc(ctx_loaded, 16)
            sp.dma_start(ctx_s, ctx_swapped_d).then_inc(ctx_loaded, 16)
            sp.dma_start(cos_t, cos_d).then_inc(ctx_loaded, 16)
            sp.dma_start(sin_t, sin_d).then_inc(ctx_loaded, 16)
            sp.dma_start(wkr, wkr_d).then_inc(wkr_loaded, 16)
            sp.dma_start(wkckv, wkckv_d).then_inc(wkckv_loaded, 16)
            for g in range(4):
                sp.dma_start(wo[:, 4 * g:4 * g + 4], wo_d[:, 4 * g:4 * g + 4]).then_inc(wo_loaded[g], 16)
            sp.dma_start(gx[:, :], gx_d.partition_broadcast(P)).then_inc(params_loaded, 16)
            sp.dma_start(gf[:, :], gf_d.partition_broadcast(P)).then_inc(params_loaded, 16)
            sp.dma_start(sg[:, :], sg_d).then_inc(params_loaded, 16)
            sp.dma_start(su[:, :], su_d).then_inc(params_loaded, 16)
            sp.dma_start(down_row[:, :], sd_d.partition_broadcast(P)).then_inc(params_loaded, 16)
            for g in range(4):
                sp.dma_start(wqr[:, 4 * g:4 * g + 4], wqr_d[:, 4 * g:4 * g + 4]).then_inc(keys_loaded[g], 16)
                sp.dma_start(wkcq[:, 4 * g:4 * g + 4], wkcq_d[:, 4 * g:4 * g + 4]).then_inc(keys_loaded[g], 16)
            for g in range(4):
                sp.dma_start(wq[:, 4 * g:4 * g + 4], wq_d[:, 4 * g:4 * g + 4]).then_inc(wq_loaded[g], 16)
            sp.wait_ge(g_scales_ready, 1)
            for g in range(B):
                sp.wait_ge(g_filled, 4 * g + 4)
                sp.dma_start(x_res[:, TPB * g:TPB * g + TPB], x_d[:, TPB * g:TPB * g + TPB]).then_inc(x_loaded[g], 16)

            for n in range(PIECES):
                if n == 1:
                    sp.wait_ge(scores_ready, 3 * TPB)
                if n >= 3:
                    sp.wait_ge(piece_cast, n - 2)
                    sp.wait_ge(piece_maxed, n - 2)
                sp.dma_start(staged(n), ffn_src[n]).then_inc(piece_loaded[n % 3], 16)
            sp.wait_ge(big_ready, 1)
            again = sp.value_load(big[0:1, 0:1], min_val=0, max_val=1)
            with sp.If(again != 0):
                sp.wait_ge(piece_cast, PIECES)
                sp.wait_ge(piece_maxed, PIECES)
                for n in range(PIECES):
                    if n >= 2:
                        sp.wait_ge(piece_split, n - 1)
                    sp.dma_start(staged_again(n), ffn_src[n]).then_inc(piece_loaded[n % 2], 16)
            with sp.Fori(0, B) as b:
                for i in range(TPB):
                    sp.wait_ge(out_ready, b * TPB + i + 1)
                    sp.dma_start(out_d[:, bass.ds(b * TPB + i, 1), :], o_sb[i].rearrange("p (a n) -> p a n", a=1)) \
                        .then_inc(out_stored[i], 16)
            for i in range(TPB):
                sp.wait_ge(out_stored[i], 16 * (B + 1))

        @block.gpsimd
        def _(pool):
            nc.gpsimd.memset(ident[:, :], 0.0).then_inc(ident_zeroed, 1)
            pool.wait_ge(ident_zeroed, 1)
            nc.gpsimd.affine_select(out=ident[:, :], in_=ident[:, :], compare_op=ALU.not_equal, fill=1.0,
                                    base=0, pattern=[[-1, P]], channel_multiplier=1).then_inc(ident_ready, 1)
            for k in range(2):
                pool.wait_ge(tensor_max, 2 * k + 2)
                nc.gpsimd.partition_all_reduce(all_max[:, 2 * k:2 * k + 2], tens_max[:, 2 * k:2 * k + 2],
                                               P, RMAX).then_inc(max_shared, 1)

            def probabilities(i, m):
                pool.wait_ge(row_inv_ready, i + 1)
                nc.gpsimd.tensor_tensor(by_head(ex[m]), by_head(ex[m]),
                                        row_inv[:, m, :].unsqueeze(2).to_broadcast([P, H, L]), ALU.mult) \
                    .then_inc(probs_ready, 1)

            with pool.Fori(0, B - 1) as g:
                for k in range(TPB):
                    probabilities(g * TPB + k, k % 2)
            for k in range(TPB):
                for n in range(3 * k, 3 * k + 3):
                    pool.wait_ge(piece_loaded[n % 3], 16 * (n // 3 + 1))
                    nc.gpsimd.tensor_scalar(w_hi(n), staged(n), -ZERO_POINT, 1.0, ALU.add, ALU.mult) \
                        .then_inc(piece_cast, 1)
                    if n % 3 == 0:
                        probabilities((B - 1) * TPB + k, k % 2)
            pool.wait_ge(tensor_max, 6)
            nc.gpsimd.partition_all_reduce(all_max[:, 4:8], tens_max[:, 4:8], P, RMAX).then_inc(max_shared, 1)
            pool.wait_ge(big_ready, 1)
            again = pool.value_load(big[0:1, 0:1], min_val=0, max_val=1)
            with pool.If(again != 0):
                pool.wait_ge(attn_ready, NT)
                pool.wait_ge(piece_cast, PIECES)
                for n in range(PIECES):
                    w, k = piece_width(n), n // 4
                    pool.wait_ge(piece_loaded[n % 2], 16 * (PIECES // 3 + n // 2 + 1))
                    if n:
                        pool.wait_ge(piece_split, n)
                    nc.gpsimd.tensor_scalar(w_tmp[:, 0:w], staged_again(n), -ZERO_POINT, w_scale[:, k:k + 1],
                                            ALU.add, ALU.mult).then_inc(tmp_ready, 1)
                    pool.wait_ge(tmp_ready, n + 1)
                    nc.gpsimd.tensor_copy(w_hi(n), w_tmp[:, 0:w]).then_inc(piece_scaled, 1)
                    pool.wait_ge(piece_scaled, n + 1)
                    nc.gpsimd.tensor_tensor(w_lo(n), w_tmp[:, 0:w], w_hi(n), ALU.subtract).then_inc(piece_split, 1)
            with pool.Fori(0, B) as b:
                for i in range(TPB):
                    pool.wait_ge(down_scaled, b * TPB + i + 1)
                    nc.gpsimd.tensor_tensor(o_sb[i], o_sb[i], x_tile(b * TPB + i), ALU.add).then_inc(out_ready, 1)

        @block.scalar
        def _(act):
            squared = [0]

            def squares_of(w, loaded, g):
                act.wait_ge(loaded[g], 16)
                if squared[0] > 0:
                    act.wait_ge(squares_ready, squared[0])
                nc.scalar.activation(junk[:, :], w[:, 4 * g:4 * g + 4, :].rearrange("p h n -> p (h n)"), ACT.Square,
                                     accum_out=part_sum[:, squared[0]:squared[0] + 1]).then_inc(squares_ready, 1)
                squared[0] += 1

            for k in range(2):
                act.wait_ge(kr_filled, k + 1)
                nc.scalar.activation(krt[:, 4 * k:4 * k + 4, :].rearrange("p q n -> p (q n)"), slot(k),
                                     ACT.Copy).then_inc(kr_copied, 1)
            for k in range(4):
                if k < 3:
                    squares_of(wo, wo_loaded, k)
                act.wait_ge(u_filled, k + 1)
                nc.scalar.activation(u_t[:, k * 1024:(k + 1) * 1024], slot(SLOT_U + k), ACT.Copy) \
                    .then_inc(u_copied, 1)
            squares_of(wo, wo_loaded, 3)
            act.wait_ge(v_scales_ready, 1)
            for v in range(2 * PAIRS):
                act.wait_ge(v_filled, v + 1)
                nc.scalar.activation(v_part(0, v), slot(SLOT_V + v), ACT.Copy, scale=s1("v_up")) \
                    .then_inc(v_hi_ready, 1)
                if v >= 12:
                    squares_of(wq, wq_loaded, v - 12)
            act.wait_ge(params_loaded, 80)
            nc.scalar.activation(s1("tanh_x"), gx[:, :], ACT.Tanh).then_inc(tanh_ready, 1)
            nc.scalar.activation(s1("tanh_f"), gf[:, :], ACT.Tanh).then_inc(tanh_ready, 1)
            for k in range(4):
                act.wait_ge(t2_filled, k + 1)
                nc.scalar.activation(t2[:, k * 1024:(k + 1) * 1024], slot(SLOT_T2 + k), ACT.Copy) \
                    .then_inc(t2_copied, 1)

            def normalise(dst, t):
                return nc.scalar.activation(dst, x_tile(t), ACT.Identity, scale=ln_scale[:, bass.ds(t, 1)],
                                            bias=ln_bias[:, bass.ds(t, 1)])

            act.wait_ge(g_scales_ready, 1)
            for h in range(H):
                act.wait_ge(g_filled, h + 1)
                nc.scalar.activation(g_all[:, 0, :, :, h * L:(h + 1) * L].rearrange("p c b l -> p (c b) l"),
                                     slot(SLOT_G + h).rearrange("p (m l) -> p m l", l=L),
                                     ACT.Copy, scale=s1("g_up")).then_inc(g_hi_ready, 1)
                if h >= H - 2:
                    act.wait_ge(ln_ready, 1)
                    normalise(xn[h % 2], h % 2).then_inc(xn_ready, 1)
            act.wait_ge(xt_filled, 1)
            nc.scalar.activation(xt[:, 0, 0].rearrange("p c t -> p (c t)"), xt_ps, ACT.Copy) \
                .then_inc(xt_hi_ready, 1)

            def attention_period(i, k, scores, probs):
                if scores:
                    act.wait_ge(xt_filled, i + 2)
                    nc.scalar.activation(xt[:, (k + 1) % 2, 0].rearrange("p c t -> p (c t)"), xt_ps, ACT.Copy) \
                        .then_inc(xt_hi_ready, 1)
                if probs:
                    act.wait_ge(pt_filled, i)
                    nc.scalar.activation(pt[:, (k + 1) % 2, 0].rearrange("p q t -> p (q t)"), pt_ps, ACT.Copy,
                                         scale=P_SCALE).then_inc(pt_hi_ready, 1)
                if scores:
                    act.wait_ge(shifted_ready, i + 1)
                    nc.scalar.activation(ex[k % 2], ex[k % 2], ACT.Exp, scale=s1("exp_scale")) \
                        .then_inc(exp_ready, 1)
                    normalise(xn[k % 2], (i + 2) % NT).then_inc(xn_ready, 1)

            for k in range(TPB):
                if k == 2:
                    act.wait_ge(ln_ready, 2)
                attention_period(k, k, True, k >= 1)
            act.wait_ge(ln_ready, B)
            with act.Fori(1, B - 1) as g:
                for k in range(TPB):
                    attention_period(g * TPB + k, k, True, True)
            act.wait_ge(ln_ready, B + 1)
            for k in range(TPB):
                attention_period((B - 1) * TPB + k, k, True, True)
                normalise(xn2[k], k).then_inc(xn2_ready, 1)

            def first_parts_of_x2t(b, ps):
                for i in range(TPB):
                    act.wait_ge(x2t_filled, b * TPB + i + 1)
                    nc.scalar.activation(x2t[:, 0, :, i * P:(i + 1) * P],
                                         ps(i).rearrange("p (c t) -> p c t", c=DCH), ACT.Copy) \
                        .then_inc(x2t_hi_ready, 1)

            act.wait_ge(piece_cast, PIECES - 2)
            act.wait_ge(piece_maxed, PIECES - 2)
            first_parts_of_x2t(0, bank)
            attention_period(NT, 0, False, True)
            act.wait_ge(ffn_scales_ready, 1)
            act.wait_ge(ln_ready, 2 * B)
            with act.Fori(0, B) as b:
                for j in range(JCH):
                    act.wait_ge(gate_filled, b * JCH + j + 1)
                    nc.scalar.activation(sil[j % 2], gate_ps(j), ACT.Silu, scale=sg[:, j:j + 1]) \
                        .then_inc(silu_ready, 1)
                    act.wait_ge(hidden_ready, b * JCH + j + 1)
                    nc.scalar.activation(h_all[:, 0, j, :], hid[j % 2], ACT.Copy).then_inc(h_hi_ready, 1)
                    if j in (1, 3, 5, 7):
                        i = j // 2
                        normalise(xn2[i], (b * TPB + TPB + i) % NT).then_inc(xn2_ready, 1)
                first_parts_of_x2t(b + 1, x2t_ps)

        @block.vector
        def _(dve):
            dve.wait_ge(ctx_loaded, 64)

            def by_batch(a):
                return a.rearrange("p (b l) -> p b l", b=B)

            nc.vector.tensor_tensor(by_batch(kvt[:, :]), by_batch(ctx_t),
                                    cos_t.unsqueeze(1).to_broadcast([P, B, L]), ALU.mult).then_inc(rope_step, 1)
            nc.vector.tensor_tensor(by_batch(ctx_s), by_batch(ctx_s),
                                    sin_t.unsqueeze(1).to_broadcast([P, B, L]), ALU.mult).then_inc(rope_step, 1)
            dve.wait_ge(rope_step, 2)
            nc.vector.tensor_tensor(kvt[:, :], kvt[:, :], ctx_s, ALU.add).then_inc(kv_ready, 1)

            maxed = [0]

            def max_of(src):
                nc.vector.tensor_reduce(part_max[:, maxed[0]:maxed[0] + 1], src, AX.X, ALU.max,
                                        apply_absolute_value=True).then_inc(piece_max, 1)
                maxed[0] += 1

            def max_of_four(k):
                dve.wait_ge(piece_max, maxed[0])
                nc.vector.tensor_reduce(tens_max[:, k:k + 1], part_max[:, maxed[0] - 4:maxed[0]], AX.X, ALU.max) \
                    .then_inc(tensor_max, 1)

            steps = [0]

            def step(instruction):
                instruction.then_inc(sc_step, 1)
                steps[0] += 1
                dve.wait_ge(sc_step, steps[0])

            def sum_of_four(k, g):
                dve.wait_ge(squares_ready, 4 * g + 4)
                nc.vector.tensor_reduce(tens_max[:, k:k + 1], part_sum[:, 4 * g:4 * g + 4], AX.X, ALU.add) \
                    .then_inc(tensor_max, 1)

            def fold_scales(first, up):
                largest, squares = all_max[:, first:first + 1], all_max[:, first + 1:first + 2]
                t0, t1 = s1("t0"), s1("t1")
                step(nc.vector.tensor_scalar(t0, largest, largest, float(DK) ** 2, ALU.mult, ALU.mult))
                step(nc.vector.tensor_scalar(t0, t0, squares, TINY, ALU.mult, ALU.max))
                step(nc.vector.tensor_scalar(t1.bitcast(INT32), t0.bitcast(INT32), 1, None, ALU.logical_shift_right))
                step(nc.vector.tensor_scalar(t1.bitcast(INT32), t1.bitcast(INT32), -1.0, float(0x5F3759DF),
                                             ALU.mult, ALU.add))
                step(nc.vector.tensor_scalar(s1(up), t1, 0.9 * TOP, None, ALU.mult))
                step(nc.vector.reciprocal(t1, s1(up)))

            for k in range(4):
                dve.wait_ge(u_copied, k + 1)
                max_of(u_t[:, k * 1024:(k + 1) * 1024])
            max_of_four(0)
            sum_of_four(1, 0)
            dve.wait_ge(max_shared, 1)
            fold_scales(0, "v_up")
            nc.vector.tensor_scalar(s1("v_down"), s1("t1"), 1.0 / P_SCALE, None, ALU.mult) \
                .then_inc(v_scales_ready, 1)

            for v in range(2 * PAIRS):
                dve.wait_ge(v_hi_ready, v + 1)
                if v == 2 * PAIRS - 2:
                    dve.wait_ge(v_filled, v + 2)
                nc.vector.scalar_tensor_tensor(out=v_part(1, v), in0=slot(SLOT_V + v), scalar=s1("v_up"),
                                               in1=v_part(0, v), op0=ALU.mult, op1=ALU.subtract) \
                    .then_inc(v_lo_ready, 1)
            for k in range(2):
                dve.wait_ge(a1_filled, k + 1)
                nc.vector.tensor_copy(a1t[:, 4 * k:4 * k + 4].rearrange("p q k -> p (q k)"),
                                      slot(SLOT_A1)[:, k * 512:(k + 1) * 512]).then_inc(a1_copied, 1)
            for k in range(4):
                dve.wait_ge(t2_copied, k + 1)
                max_of(t2[:, k * 1024:(k + 1) * 1024])
            max_of_four(2)
            sum_of_four(3, 1)
            dve.wait_ge(max_shared, 2)
            fold_scales(2, "g_up")
            nc.vector.tensor_scalar(s1("exp_scale"), s1("t1"), 1.0 / X_SCALE, None, ALU.mult) \
                .then_inc(g_scales_ready, 1)
            dve.wait_ge(tanh_ready, 2)
            step(nc.vector.tensor_tensor(s1("attn_gain"), s1("tanh_x"), s1("v_down"), ALU.mult))

            NEWTONS = 3
            LN_STEPS = 3 + 4 * NEWTONS + 1

            def normalisation(call, first, meanvar):
                v, y, c = (newton[:, m, :] for m in range(3))
                scale, bias = ln_scale[:, bass.ds(first, TPB)], ln_bias[:, bass.ds(first, TPB)]
                mean = meanvar[:, :, 0:1].rearrange("p t a -> p (t a)")
                var = meanvar[:, :, 1:2].rearrange("p t a -> p (t a)")
                done = [0]

                def after(instruction):
                    instruction.then_inc(ln_step, 1)
                    done[0] += 1
                    dve.wait_ge(ln_step, call * LN_STEPS + done[0])

                after(nc.vector.tensor_scalar(v, var, EPS, None, ALU.add))
                after(nc.vector.tensor_scalar(y.bitcast(INT32), v.bitcast(INT32), 1, None, ALU.logical_shift_right))
                after(nc.vector.tensor_scalar(y.bitcast(INT32), y.bitcast(INT32), -1.0, float(0x5F3759DF),
                                              ALU.mult, ALU.add))
                for _ in range(NEWTONS):
                    after(nc.vector.tensor_tensor(c, y, y, ALU.mult))
                    after(nc.vector.tensor_tensor(c, c, v, ALU.mult))
                    after(nc.vector.tensor_scalar(c, c, -0.5, 1.5, ALU.mult, ALU.add))
                    after(nc.vector.tensor_tensor(y, y, c, ALU.mult))
                after(nc.vector.tensor_scalar(scale, y, X_SCALE, None, ALU.mult))
                nc.vector.scalar_tensor_tensor(out=bias, in0=mean, scalar=-1.0, in1=scale,
                                               op0=ALU.mult, op1=ALU.mult).then_inc(ln_ready, 1)

            def x_statistics(t):
                dve.wait_ge(x_loaded[t // TPB], 16)
                nc.vector.bn_stats(x_stats[:, t % TPB, :], x_tile(t)).then_inc(stats_ready, 1)
                dve.wait_ge(stats_ready, t + 1)
                nc.vector.bn_aggr(x_meanvar[:, t % TPB, :], x_stats[:, t % TPB, :]).then_inc(meanvar_ready, 1)
                if t % TPB == TPB - 1:
                    dve.wait_ge(meanvar_ready, t + 1)
                    normalisation(t // TPB, t - TPB + 1, x_meanvar)

            for h in range(H):
                dve.wait_ge(g_hi_ready, h + 1)
                nc.vector.scalar_tensor_tensor(
                    out=g_all[:, 1, :, :, h * L:(h + 1) * L].rearrange("p c b l -> p (c b) l"),
                    in0=slot(SLOT_G + h).rearrange("p (m l) -> p m l", l=L), scalar=s1("g_up"),
                    in1=g_all[:, 0, :, :, h * L:(h + 1) * L].rearrange("p c b l -> p (c b) l"),
                    op0=ALU.mult, op1=ALU.subtract).then_inc(g_lo_ready, 1)
                if 8 <= h < 8 + TPB:
                    x_statistics(h - 8)

            def hold():
                dve.wait_ge(tanh_ready, 2)

            def attention_period(i, k, scores, probs, attn):
                m = k % 2
                if scores:
                    dve.wait_ge(scores_ready, i + 1)
                    nc.vector.tensor_reduce(row_max[:, m, :], by_head(scores_ps(k)), AX.X, ALU.max) \
                        .then_inc(row_max_ready, 1)
                    dve.wait_ge(row_max_ready, i + 1)
                    nc.vector.tensor_tensor(by_head(ex[m]), by_head(scores_ps(k)),
                                            row_max[:, m, :].unsqueeze(2).to_broadcast([P, H, L]),
                                            ALU.subtract).then_inc(shifted_ready, 1)
                    dve.wait_ge(xt_hi_ready, i + 2)
                    nc.vector.tensor_tensor(xt[:, (k + 1) % 2, 1].rearrange("p c t -> p (c t)"), xt_ps,
                                            xt[:, (k + 1) % 2, 0].rearrange("p c t -> p (c t)"),
                                            ALU.subtract).then_inc(xt_lo_ready, 1)
                if probs:
                    dve.wait_ge(pt_hi_ready, i)
                    nc.vector.scalar_tensor_tensor(out=pt[:, (k + 1) % 2, 1].rearrange("p q t -> p (q t)"),
                                                   in0=pt_ps, scalar=P_SCALE,
                                                   in1=pt[:, (k + 1) % 2, 0].rearrange("p q t -> p (q t)"),
                                                   op0=ALU.mult, op1=ALU.subtract).then_inc(pt_lo_ready, 1)
                if scores:
                    dve.wait_ge(exp_ready, i + 1)
                    nc.vector.tensor_reduce(row_sum[:, m, :], by_head(ex[m]), AX.X, ALU.add) \
                        .then_inc(row_sum_ready, 1)
                    dve.wait_ge(row_sum_ready, i + 1)
                    nc.vector.reciprocal(row_inv[:, m, :], row_sum[:, m, :]).then_inc(row_inv_ready, 1)
                if attn:
                    dve.wait_ge(attn_ready, i - 1)
                    nc.vector.scalar_tensor_tensor(out=x_tile(i - 2), in0=out_ps, scalar=s1("attn_gain"),
                                                   in1=x_tile(i - 2), op0=ALU.mult, op1=ALU.add) \
                        .then_inc(x1_ready, 1)
                    hold()
                    dve.wait_ge(x1_ready, i - 1)
                    nc.vector.bn_stats(stats[:, (k + 2) % TPB, :], x_tile(i - 2)).then_inc(x1_stats_ready, 1)
                    hold()
                    dve.wait_ge(x1_stats_ready, i - 1)
                    nc.vector.bn_aggr(meanvar[:, (k + 2) % TPB, :], stats[:, (k + 2) % TPB, :]) \
                        .then_inc(x1_meanvar_ready, 1)

            def batch_normalisation(g):
                dve.wait_ge(x1_meanvar_ready, g * TPB)
                normalisation(B - 1 + g, (g - 1) * TPB, meanvar)

            def maxima_of_pieces(n0, n1):
                for n in range(n0, n1):
                    dve.wait_ge(piece_loaded[n % 3], 16 * (n // 3 + 1))
                    nc.vector.tensor_reduce(ffn_max[:, n:n + 1], staged(n), AX.X, ALU.max,
                                            apply_absolute_value=True).then_inc(piece_maxed, 1)

            dve.wait_ge(xt_hi_ready, 1)
            nc.vector.tensor_tensor(xt[:, 0, 1].rearrange("p c t -> p (c t)"), xt_ps,
                                    xt[:, 0, 0].rearrange("p c t -> p (c t)"), ALU.subtract) \
                .then_inc(xt_lo_ready, 1)
            for k in range(TPB):
                attention_period(k, k, True, k >= 1, k >= 2)
                for t in range(TPB + 3 * k, TPB + 3 * k + 3):
                    x_statistics(t)
            with dve.Fori(1, B - 1) as g:
                for k in range(TPB):
                    attention_period(g * TPB + k, k, True, True, True)
                    if k == 1:
                        batch_normalisation(g)
            for k in range(TPB):
                i = (B - 1) * TPB + k
                attention_period(i, k, True, True, True)
                if k == 1:
                    batch_normalisation(B - 1)
                maxima_of_pieces(3 * k, 3 * k + 3)

            def second_parts_of_x2t(b, ps):
                for i in range(TPB):
                    dve.wait_ge(x2t_hi_ready, b * TPB + i + 1)
                    nc.vector.tensor_tensor(x2t[:, 1, :, i * P:(i + 1) * P],
                                            ps(i).rearrange("p (c t) -> p c t", c=DCH),
                                            x2t[:, 0, :, i * P:(i + 1) * P], ALU.subtract) \
                        .then_inc(x2t_lo_ready, 1)

            second_parts_of_x2t(0, bank)
            attention_period(NT, 0, False, True, True)

            step(nc.vector.tensor_tensor(sgsu[:, :], sg[:, :], su[:, :], ALU.mult))
            nc.vector.tensor_reduce(tens_max[:, 7:8], sgsu[:, :], AX.X, ALU.max,
                                    apply_absolute_value=True).then_inc(tensor_max, 1)
            dve.wait_ge(piece_maxed, PIECES)
            nc.vector.tensor_reduce(tens_max[:, 4:7], ffn_max[:, :].rearrange("p (m n) -> p m n", m=3),
                                    AX.X, ALU.max).then_inc(tensor_max, 1)
            dve.wait_ge(max_shared, 3)
            step(nc.vector.tensor_scalar(w_big, all_max[:, 4:7], EXACT - ZERO_POINT, None, ALU.is_gt))
            step(nc.vector.tensor_reduce(s1("t0"), w_big, AX.X, ALU.max))
            nc.vector.tensor_copy(big[:, :], s1("t0")).then_inc(big_ready, 1)
            step(nc.vector.tensor_scalar(w_bound, all_max[:, 4:7], ZERO_POINT, None, ALU.add))
            step(nc.vector.reciprocal(w_scale, w_bound))
            step(nc.vector.tensor_scalar(w_scale, w_scale, EXACT, 1.0, ALU.mult, ALU.subtract))
            step(nc.vector.tensor_tensor(w_scale, w_scale, w_big, ALU.mult))
            step(nc.vector.tensor_scalar(w_scale, w_scale, 1.0, None, ALU.add))
            step(nc.vector.reciprocal(w_inv, w_scale))
            step(nc.vector.tensor_tensor(s1("t0"), w_bound[:, 0:1], w_bound[:, 1:2], ALU.mult))
            step(nc.vector.tensor_tensor(s1("t0"), s1("t0"), all_max[:, 7:8], ALU.mult))
            step(nc.vector.tensor_scalar(s1("h_bound"), s1("t0"), float(D) * D, TINY, ALU.mult, ALU.max))
            step(nc.vector.reciprocal(s1("t1"), s1("h_bound")))
            step(nc.vector.tensor_scalar(s1("gate_k"), w_inv[:, 0:1], 1.0 / X_SCALE, None, ALU.mult))
            step(nc.vector.tensor_scalar(s1("up_k"), w_inv[:, 1:2], s1("t1"), TOP / X_SCALE, ALU.mult, ALU.mult))
            step(nc.vector.tensor_scalar(s1("down_k"), w_inv[:, 2:3], s1("h_bound"), 1.0 / TOP, ALU.mult, ALU.mult))
            step(nc.vector.tensor_tensor(s1("down_k"), s1("down_k"), s1("tanh_f"), ALU.mult))
            step(nc.vector.tensor_scalar(sg[:, :], sg[:, :], s1("gate_k"), None, ALU.mult))
            step(nc.vector.tensor_scalar(su[:, :], su[:, :], s1("up_k"), None, ALU.mult))
            nc.vector.tensor_scalar(down_row[:, :], down_row[:, :], s1("down_k"), None, ALU.mult) \
                .then_inc(ffn_scales_ready, 1)

            attention_period(NT + 1, 1, False, False, True)
            batch_normalisation(B)
            for i in range(TPB):
                dve.sem_inc(out_stored[i], 16)
            dve.wait_ge(ffn_scales_ready, 1)
            with dve.Fori(0, B) as b:
                for j in range(JCH):
                    dve.wait_ge(up_filled, b * JCH + j + 1)
                    dve.wait_ge(silu_ready, b * JCH + j + 1)
                    nc.vector.scalar_tensor_tensor(out=hid[j % 2], in0=up_ps(j), scalar=su[:, j:j + 1],
                                                   in1=sil[j % 2], op0=ALU.mult, op1=ALU.mult) \
                        .then_inc(hidden_ready, 1)
                    dve.wait_ge(h_hi_ready, b * JCH + j + 1)
                    nc.vector.tensor_tensor(h_all[:, 1, j, :], hid[j % 2], h_all[:, 0, j, :], ALU.subtract) \
                        .then_inc(h_lo_ready, 1)
                second_parts_of_x2t(b + 1, x2t_ps)
                for i in range(TPB):
                    dve.wait_ge(down_filled, b * TPB + i + 1)
                    dve.wait_ge(out_stored[i], 16 * (b + 1))
                    nc.vector.tensor_tensor(o_sb[i], down_ps(i), down_row[:, :], ALU.mult).then_inc(down_scaled, 1)

        @block.tensor
        def _(pe):
            pe.wait_ge(wkr_loaded, 16)
            pe.wait_ge(kv_ready, 1)
            for q in range(PAIRS):
                last = nc.tensor.matmul(psum[:, q * BL:(q + 1) * BL], wkr[:, q * P:(q + 1) * P], kvt[:, :],
                                        start=True, stop=True)
                if q % 4 == 3:
                    last.then_inc(kr_filled, 1)
            pe.wait_ge(wkckv_loaded, 16)
            for h in range(H):
                if h in (8, 12):
                    pe.wait_ge(kr_copied, h // 4 - 1)
                last = nc.tensor.matmul(slot(SLOT_U + h // 4)[:, (h % 4) * BL:(h % 4 + 1) * BL],
                                        wkckv[:, h * DK:(h + 1) * DK], kvt[:, :], start=True, stop=True)
                if h % 4 == 3:
                    last.then_inc(u_filled, 1)
            pe.wait_ge(u_copied, 4)
            for v in range(2 * PAIRS):
                q = v // 2
                if v % 4 == 0:
                    pe.wait_ge(wo_loaded[v // 4], 16)
                if v >= 4:
                    pe.wait_ge(v_lo_ready, v - 3)
                for m in range(2):
                    b = v % 2 * 2 + m
                    for h in (2 * q, 2 * q + 1):
                        half = (h % 2) * L
                        at_u = h * BL + b * L
                        last = nc.tensor.matmul(slot(SLOT_V + v)[half:half + L, m * D:(m + 1) * D],
                                                u_t[:, at_u:at_u + L], wo[:, h, :], start=True, stop=True)
                last.then_inc(v_filled, 1)
            pe.wait_ge(v_lo_ready, 2 * PAIRS - 3)
            for q in range(PAIRS):
                if q % 2 == 0:
                    pe.wait_ge(keys_loaded[q // 2], 32)
                for c in range(QCH):
                    for h in (2 * q, 2 * q + 1):
                        half = (h % 2) * R
                        last = nc.tensor.matmul(slot(SLOT_A1)[half:half + R, q * DK:(q + 1) * DK],
                                                wqr[:, h, c, :], wkcq[:, h, c, :],
                                                start=c == 0, stop=c == QCH - 1)
                if q % 4 == 3:
                    last.then_inc(a1_filled, 1)
            for h in range(H):
                if h % 8 == 0:
                    pe.wait_ge(a1_copied, h // 8 + 1)
                if h % 4 == 0 and h < 12:
                    pe.wait_ge(v_lo_ready, 2 * PAIRS - 2 + h // 4)
                elif h == 12:
                    pe.wait_ge(a1_copied, 2)
                half = (h % 2) * R
                at_h = (t2_at(h) % 4) * BL
                last = nc.tensor.matmul(slot(SLOT_T2 + h // 4)[:, at_h:at_h + BL], a1t[half:half + R, h // 2, :],
                                        krt[half:half + R, h // 2, :], start=True, stop=True)
                if h % 4 == 3:
                    last.then_inc(t2_filled, 1)
            for h in range(H):
                if h % 4 == 0:
                    pe.wait_ge(wq_loaded[h // 4], 16)
                if h < 4:
                    pe.wait_ge(t2_copied, max(h + 1, t2_at(h) // 4 + 1))
                else:
                    pe.wait_ge(g_lo_ready, h - 3)
                for c in range(DCH):
                    last = nc.tensor.matmul(slot(SLOT_G + h)[:, c * BL:(c + 1) * BL], wq[:, h, c * P:(c + 1) * P],
                                            t2[:, t2_at(h) * BL:(t2_at(h) + 1) * BL], start=True, stop=True)
                last.then_inc(g_filled, 1)

            def transpose_rows(dst, src):
                for c in range(DCH):
                    last = nc.tensor.transpose(dst[:, c * P:(c + 1) * P], src[:, c * P:(c + 1) * P], ident[:, :])
                return last

            def g_at(s, c, b, n):
                return g_region[:, bass.ds((s * DCH + c) * B * HL + b * HL + n * 512, 512)]

            def v_at(q, s, b):
                return v_region[:, bass.ds((q * 2 + s) * B * D + b * D, D)]

            def attention_period(i, k, b, scores, probs, attn):
                if scores:
                    pe.wait_ge(xt_lo_ready, i + 1)
                    if not isinstance(i, int) or i >= 2:
                        pe.wait_ge(shifted_ready, i - 1)
                    m = k % 2
                    for c in range(DCH):
                        for sx, sy in ((0, 0), (0, 1), (1, 0)):
                            for n in range(HL // 512):
                                last = nc.tensor.matmul(scores_ps(k)[:, n * 512:(n + 1) * 512], xt[:, m, sx, c, :],
                                                        g_at(sy, c, b, n), start=c == 0 and sx + sy == 0,
                                                        stop=c == DCH - 1 and sx == 1)
                    last.then_inc(scores_ready, 1)
                    pe.wait_ge(xn_ready, i + 2)
                    transpose_rows(xt_ps, xn[(k + 1) % 2]).then_inc(xt_filled, 1)
                if probs:
                    pe.wait_ge(probs_ready, i)
                    if not isinstance(i, int) or i >= 2:
                        pe.wait_ge(pt_lo_ready, i - 1)
                    for q in range(PAIRS):
                        last = nc.tensor.transpose(pt_ps[:, q * P:(q + 1) * P],
                                                   ex[(k + 1) % 2][:, q * P:(q + 1) * P], ident[:, :])
                    last.then_inc(pt_filled, 1)
                if attn:
                    pe.wait_ge(pt_lo_ready, i - 1)
                    if not isinstance(i, int) or i >= 3:
                        pe.wait_ge(x1_ready, i - 2)
                    bb = b if k % TPB >= 2 else b - 1
                    for q in range(PAIRS):
                        for sx, sy in ((0, 0), (0, 1), (1, 0)):
                            last = nc.tensor.matmul(out_ps, pt[:, k % 2, sx, q, :], v_at(q, sy, bb),
                                                    start=q == 0 and sx + sy == 0,
                                                    stop=q == PAIRS - 1 and sx == 1)
                    last.then_inc(attn_ready, 1)

            pe.wait_ge(ident_ready, 1)
            pe.wait_ge(xn_ready, 1)
            pe.wait_ge(g_lo_ready, H - 3)
            transpose_rows(xt_ps, xn[0]).then_inc(xt_filled, 1)
            pe.wait_ge(g_lo_ready, H)
            for k in range(TPB):
                attention_period(k, k, 0, True, k >= 1, k >= 2)
            with pe.Fori(1, B) as g:
                for k in range(TPB):
                    attention_period(g * TPB + k, k, g, True, True, True)

            def transpose_batch(b, ps):
                for i in range(TPB):
                    pe.wait_ge(xn2_ready, b * TPB + i + 1)
                    transpose_rows(ps(i), xn2[i]).then_inc(x2t_filled, 1)

            def feed_forward(parts):
                with pe.Fori(0, B) as b:
                    pe.wait_ge(x2t_lo_ready, b * TPB + TPB)
                    for j in range(JCH):
                        for first, ps, filled, freed in ((0, gate_ps(j), gate_filled, silu_ready),
                                                         (DCH, up_ps(j), up_filled, hidden_ready)):
                            if j >= 2:
                                pe.wait_ge(freed, b * JCH + j - 1)
                            for c in range(DCH):
                                for sx, w in parts:
                                    last = nc.tensor.matmul(ps, w(first + c)[:, j * P:(j + 1) * P], x2t[:, sx, c, :],
                                                            start=c == 0 and (sx, w) == parts[0],
                                                            stop=c == DCH - 1 and (sx, w) == parts[-1])
                            last.then_inc(filled, 1)
                    pe.wait_ge(silu_ready, b * JCH + JCH - 1)
                    pe.wait_ge(hidden_ready, b * JCH + JCH - 1)
                    transpose_batch(b + 1, x2t_ps)
                    pe.wait_ge(h_lo_ready, b * JCH + JCH - 1)
                    for i in range(TPB):
                        if i >= 2:
                            pe.wait_ge(down_scaled, b * TPB + i - 1)
                        for j in range(JCH):
                            n, m = down_piece(j)
                            if i == 0 and j == JCH - 1:
                                pe.wait_ge(h_lo_ready, b * JCH + JCH)
                            for sx, w in parts:
                                last = nc.tensor.matmul(down_ps(i), h_all[:, sx, j, i * P:(i + 1) * P],
                                                        w(8 + n)[:, m * D:(m + 1) * D],
                                                        start=j == 0 and (sx, w) == parts[0],
                                                        stop=j == JCH - 1 and (sx, w) == parts[-1])
                        last.then_inc(down_filled, 1)

            pe.wait_ge(shifted_ready, NT)
            transpose_batch(0, bank)
            attention_period(NT, 0, B, False, True, True)
            attention_period(NT + 1, 1, B, False, False, True)
            pe.wait_ge(pt_lo_ready, NT)
            pe.wait_ge(xt_lo_ready, NT + 1)
            pe.wait_ge(piece_cast, PIECES)
            pe.wait_ge(big_ready, 1)
            general = pe.value_load(big[0:1, 0:1], min_val=0, max_val=1)
            with pe.If(general != 0):
                pe.wait_ge(piece_split, PIECES)
                feed_forward([(0, w_hi), (0, w_lo), (1, w_hi)])
            with pe.Else():
                feed_forward([(0, w_hi), (1, w_hi)])


def kernel(x, ctx_512, g_xattn, g_ffn, L0_xattn_Wq, L0_xattn_w_kc_q, L0_xattn_w_kc_kv, L0_xattn_W_qr,
           L0_xattn_W_kr, L0_xattn_Wo, L0_ffn_wq_gate, L0_ffn_s_gate, L0_ffn_wq_up, L0_ffn_s_up,
           L0_ffn_wq_down, L0_ffn_s_down):
    import numpy as np
    import concourse.bacc as bacc
    from concourse.bass_utils import run_bass_kernel_spmd

    inv_freq = (1.0 / np.float32(10000.0) ** (np.arange(0, DC, 2, dtype=np.float32) / np.float32(DC)))
    freqs = np.arange(L, dtype=np.float32)[:, None] * inv_freq.astype(np.float32)[None, :]
    cos = np.repeat(np.cos(freqs), 2, axis=-1).T
    sin = np.repeat(np.sin(freqs), 2, axis=-1).T
    sign = np.where(np.arange(DC) < DC // 2, -1.0, 1.0).astype(np.float32)[:, None]

    a = {k: np.asarray(v) for k, v in dict(
        x=x, ctx=ctx_512, gx=g_xattn, gf=g_ffn, wq=L0_xattn_Wq, wkcq=L0_xattn_w_kc_q, wkckv=L0_xattn_w_kc_kv,
        wqr=L0_xattn_W_qr, wkr=L0_xattn_W_kr, wo=L0_xattn_Wo, wg=L0_ffn_wq_gate, wu=L0_ffn_wq_up,
        wd=L0_ffn_wq_down, sg=L0_ffn_s_gate, su=L0_ffn_s_up, sd=L0_ffn_s_down).items()}
    ctx_t = a["ctx"].reshape(BL, DC).T
    laid = [
        ("x", a["x"].reshape(NT, P, D).transpose(1, 0, 2)),
        ("ctx_t", ctx_t),
        ("ctx_swapped", np.concatenate([ctx_t[DC // 2:], ctx_t[:DC // 2]])),
        ("cos", cos.astype(np.float32)),
        ("sin", (sin * sign).astype(np.float32)),
        ("gx", a["gx"]),
        ("gf", a["gf"]),
        ("wq", a["wq"].reshape(H, DK, D).transpose(1, 0, 2)),
        ("wkcq", a["wkcq"].reshape(H, DK, QCH, P).transpose(3, 0, 2, 1)),
        ("wkckv", a["wkckv"].transpose(2, 0, 1).reshape(DC, H * DK)),
        ("wqr", a["wqr"].reshape(H, QCH, P, R).transpose(2, 0, 1, 3)),
        ("wkr", a["wkr"].transpose(1, 0, 2).reshape(DC, H * R)),
        ("wo", a["wo"].T.reshape(H, DK, D).transpose(1, 0, 2)),
        ("wg", a["wg"].T.reshape(DCH, P, HID).transpose(1, 0, 2)),
        ("wu", a["wu"].T.reshape(DCH, P, HID).transpose(1, 0, 2)),
        ("wd", a["wd"].T.reshape(JCH, P, D).transpose(1, 0, 2).reshape(P, JCH * D)),
        ("sg", a["sg"].reshape(JCH, P).T),
        ("su", a["su"].reshape(JCH, P).T),
        ("sd", a["sd"]),
    ]
    nc = bacc.Bacc("TRN2", target_bir_lowering=False, num_devices=1)
    arrays, aps = {}, []
    for name, v in laid:
        v = np.ascontiguousarray(v)
        arrays[f"in_{name}"] = v
        aps.append(nc.dram_tensor(f"in_{name}", v.shape, mybir.dt.from_np(v.dtype), kind="ExternalInput").ap())
    aps.append(nc.dram_tensor("out_0", (P, NT, D), FP32, kind="ExternalOutput").ap())
    gated_block(nc, *aps)
    r = run_bass_kernel_spmd(nc, [arrays], core_ids=[0])
    out = r.results[0]["out_0"]
    return np.ascontiguousarray(np.asarray(out).transpose(1, 0, 2)).reshape(B, S, D)
```

```python
import concourse.bass as bass
from concourse import mybir
from contextlib import ExitStack

FP32 = mybir.dt.float32
FP16 = mybir.dt.float16
INT32 = mybir.dt.int32
ALU = mybir.AluOpType
ACT = mybir.ActivationFunctionType
AX = mybir.AxisListType
RMAX = bass.bass_isa.ReduceOp.max

P = 128
B, S, D = 4, 512, 512
H, L = 16, 64
DK = 128
DC = 128
CQ = 384
R = 64
HID = 1408
DCH = D // P
QCH = CQ // P
JCH = HID // P
TPB = S // P
NT = B * TPB
PAIRS = H // 2
BL = B * L
HL = H * L
EPS = 1e-5
ZERO_POINT = 128.0

X_SCALE = 256.0
P_SCALE = 4096.0
TOP = 32768.0
EXACT = 2048.0
TINY = 1e-30

W_COLS = DCH * HID
PIECE = HL
PPW = -(-W_COLS // PIECE)
PIECES = 3 * PPW
PIECES_OF_PERIOD = ((0, 1), (), (2, 3), (4, 5))


def piece_width(r):
    return min(PIECE, W_COLS - r * PIECE)


WARM_UPS = 19

WO_PARTS = ((0, 4), (4, 8), (8, 12), (12, 14), (14, 16))
WQ_PARTS = ((0, 4), (4, 8), (8, 12), (12, 16))


def t2_at(h):
    return (h // 4) * 4 + (h % 2) * 2 + (h // 2) % 2


def gated_block(nc, x_d, ctx_d, ctx_swapped_d, cos_d, sin_d, gx_d, gf_d, wq_d, wkcq_d, wkckv_d,
                wqr_d, wkr_d, wo_d, wffn_d, sg_d, su_d, sd_d, out_d):
    ctx = ExitStack()
    with ctx:
        def sb(name, shape, dt):
            return ctx.enter_context(nc.sbuf_tensor(name, shape, dt))

        def sem(name):
            return ctx.enter_context(nc.semaphore(name))

        g_region = sb("g_region", [P, 2 * DCH * B * HL], FP16)
        v_region = sb("v_region", [P, PAIRS * 2 * B * D], FP16)
        x_res = sb("x_res", [P, NT, D], FP32)
        work = sb("work", [P, 8192], FP32)
        ident = sb("ident", [P, P], FP32)
        kvt = sb("kvt", [P, BL], FP32)
        down_row = sb("down_row", [P, D], FP32)
        sg = sb("sg", [P, JCH], FP32)
        su = sb("su", [P, JCH], FP32)
        sgsu = sb("sgsu", [P, JCH], FP32)
        gx = sb("gx", [P, 1], FP32)
        gf = sb("gf", [P, 1], FP32)
        x_stats = sb("x_stats", [P, TPB, 6], FP32)
        x1_stats = sb("x1_stats", [P, TPB, 6], FP32)
        meanvar = sb("meanvar", [P, 2, TPB, 2], FP32)
        ln_scale = sb("ln_scale", [P, NT], FP32)
        ln_bias = sb("ln_bias", [P, NT], FP32)
        newton = sb("newton", [P, 3, 2, TPB], FP32)
        spare = sb("spare", [P, TPB * D], FP32)
        row_max = sb("row_max", [P, 2, H], FP32)
        row_sum = sb("row_sum", [P, 2, H], FP32)
        row_inv = sb("row_inv", [P, 2, H], FP32)
        part_max = sb("part_max", [P, 8], FP32)
        tens_max = sb("tens_max", [P, 8], FP32)
        all_max = sb("all_max", [P, 8], FP32)
        ffn_max = sb("ffn_max", [P, PIECES], FP32)
        part_sum = sb("part_sum", [P, len(WO_PARTS) + len(WQ_PARTS)], FP32)
        sc = sb("sc", [P, 32], FP32)
        less_zero = sb("less_zero", [P, 1], FP32)
        big = sb("big", [P, 1], INT32)

        g_all = g_region[:, :].rearrange("p (s c b n) -> p s c b n", s=2, c=DCH, b=B)
        v_all = v_region[:, :].rearrange("p (q s b n) -> p q s b n", q=PAIRS, s=2, b=B)
        g32 = g_region[:, :].bitcast(FP32)
        at = 0
        wkcq = g32[:, at:at + H * QCH * DK].rearrange("p (h c k) -> p h c k", h=H, c=QCH)
        at += H * QCH * DK
        wqr = g32[:, at:at + H * QCH * R].rearrange("p (h c r) -> p h c r", h=H, c=QCH)
        at += H * QCH * R
        wkr = g32[:, at:at + H * R]
        at += H * R
        wkckv = g32[:, at:at + H * DK]
        at += H * DK
        ctx_t = g32[:, at:at + BL]
        ctx_s = g32[:, at + BL:at + 2 * BL]
        cos_t = g32[:, at + 2 * BL:at + 2 * BL + L]
        sin_t = g32[:, at + 2 * BL + L:at + 2 * BL + 2 * L]
        at_end = at + 2 * BL + 2 * L
        v32 = v_region[:, :].bitcast(FP32)
        wq = x_res
        wo = v32[:, H * D:2 * H * D].rearrange("p (h n) -> p h n", h=H)

        t2 = work[:, 0:H * BL]
        ex = [work[:, i * HL:(i + 1) * HL] for i in range(2)]
        x2t = work[:, 2048:4096].bitcast(FP16).rearrange("p (s c t) -> p s c t", s=2, c=DCH)
        u_t = work[:, 4096:8192]
        pt = work[:, 4096:6144].bitcast(FP16).rearrange("p (i s q t) -> p i s q t", i=2, s=2, q=PAIRS)
        xn = [work[:, 6144 + i * D:6144 + (i + 1) * D] for i in range(2)]
        xt = work[:, 7168:8192].bitcast(FP16).rearrange("p (i s c t) -> p i s c t", i=2, s=2, c=DCH)
        sil = [work[:, 4096 + i * S:4096 + (i + 1) * S] for i in range(2)]
        hid = [work[:, 5120 + i * S:5120 + (i + 1) * S] for i in range(2)]
        o_sb = [work[:, 6144 + i * D:6144 + (i + 1) * D] for i in range(TPB)]
        junk = g_region[:, 2 * at_end:2 * at_end + 4 * D]
        a1t = g32[:, at_end + 2 * D:at_end + 2 * D + PAIRS * DK].rearrange("p (q k) -> p q k", q=PAIRS)
        krt = spare[:, :].rearrange("p (q n) -> p q n", q=PAIRS)
        xn2 = [spare[:, i * D:(i + 1) * D] for i in range(TPB)]

        def w_hi(m, r):
            return g_region[:, bass.ds(r * B * HL + m * HL, piece_width(r))]

        def staged(r):
            return work[:, 2048 + r % 2 * PIECE:2048 + r % 2 * PIECE + piece_width(r)].bitcast(INT32)

        def staged_again(r):
            at_r = (PPW + r % 2) * B * HL
            return g_region[:, at_r:at_r + 2 * piece_width(r)].bitcast(INT32)

        def w_lo(m, r):
            return v_region[:, (m * PPW + r) * PIECE:(m * PPW + r) * PIECE + piece_width(r)]

        def columns(part, m, at_w, width):
            return part(m, at_w // PIECE)[:, at_w % PIECE:at_w % PIECE + width]

        at = PIECES * PIECE
        h_all = v_region[:, at:at + 2 * JCH * S].rearrange("p (s j t) -> p s j t", s=2, j=JCH)
        at += 2 * JCH * S
        w_tmp = v_region[:, at:at + 2 * PIECE].bitcast(FP32)

        def piece_source(m, r):
            return wffn_d[:, bass.ds(m, 1), r * PIECE:r * PIECE + piece_width(r)].rearrange("p a n -> p (a n)")

        psum = ctx.enter_context(nc.psum_tensor("psum", [P, 4096], FP32))

        def slot(n):
            return psum[:, ((n + 3) % 4) * 1024:((n + 3) % 4 + 1) * 1024]

        def scores_ps(i):
            return psum[:, (i % 2) * HL:(i % 2 + 1) * HL]

        pt_ps = psum[:, 2048:3072]
        out_ps = psum[:, 3072:3584]
        xt_ps = psum[:, 3584:4096]

        def rows_ps(t):
            return out_ps if isinstance(t, int) and t == 1 else xt_ps

        def gate_ps(j):
            return psum[:, (j % 2) * 512:(j % 2) * 512 + S]

        def up_ps(j):
            return psum[:, 1024 + (j % 2) * 512:1024 + (j % 2) * 512 + S]

        def bank(i):
            return psum[:, i * 512:(i + 1) * 512]

        def x2t_ps(i):
            return bank((4, 5, (JCH - 2) % 2, 2 + (JCH - 2) % 2)[i])

        def down_ps(i):
            return psum[:, 3072 + (i % 2) * 512:3072 + (i % 2) * 512 + D]

        def last_ps(n):
            return (bank(0), down_ps(TPB - 1))[n]

        names = ["g_up", "exp_scale", "v_up", "v_down", "tanh_x", "tanh_f",
                 "attn_gain", "t0", "t1", "h_bound", "h_up", "gate_k", "up_k", "down_k"]

        def s1(name):
            i = names.index(name)
            return sc[:, i:i + 1]

        w_scale = sc[:, 20:23]
        w_inv = sc[:, 23:26]
        w_bound = sc[:, 26:29]
        w_big = sc[:, 29:32]

        ctx_loaded = sem("ctx_loaded")
        wkr_loaded = [sem(f"wkr_loaded{q}") for q in range(2)]
        keys_loaded = [sem(f"keys_loaded{g}") for g in range(4)]
        wkckv_loaded = sem("wkckv_loaded")
        wq_loaded = [sem(f"wq_loaded{g}") for g in range(4)]
        wo_loaded = [sem(f"wo_loaded{g}") for g in range(len(WO_PARTS))]
        first_x_loaded = [sem(f"first_x_loaded{t}") for t in range(TPB)]
        x_loaded = [None] + [sem(f"x_loaded{g}") for g in range(1, B)]
        params_loaded = sem("params_loaded")
        piece_loaded = [sem(f"piece_loaded{k}") for k in range(2)]
        out_stored = [sem(f"out_stored{k}") for k in range(TPB)]
        pool_constants = sem("pool_constants")
        ident_ready = sem("ident_ready")
        rope_step = sem("rope_step")
        kv_ready = sem("kv_ready")
        kr_filled = sem("kr_filled")
        kr_copied = sem("kr_copied")
        a1_filled = sem("a1_filled")
        a1_copied = sem("a1_copied")
        t2_filled = sem("t2_filled")
        t2_copied = sem("t2_copied")
        u_filled = sem("u_filled")
        u_copied = sem("u_copied")
        g_filled = sem("g_filled")
        g_hi_ready = sem("g_hi_ready")
        g_lo_ready = sem("g_lo_ready")
        v_filled = sem("v_filled")
        v_hi_ready = sem("v_hi_ready")
        v_lo_ready = sem("v_lo_ready")
        piece_max = sem("piece_max")
        squares_ready = sem("squares_ready")
        tensor_max = sem("tensor_max")
        max_shared = sem("max_shared")
        sc_step = sem("sc_step")
        g_scales_ready = sem("g_scales_ready")
        exp_scale_ready = sem("exp_scale_ready")
        v_scales_ready = sem("v_scales_ready")
        ffn_scales_ready = sem("ffn_scales_ready")
        big_ready = sem("big_ready")
        tanh_ready = sem("tanh_ready")
        stats_ready = sem("stats_ready")
        late_stats_ready = [sem(f"late_stats_ready{m}") for m in range(TPB)]
        meanvar_ready = sem("meanvar_ready")
        x1_stats_ready = sem("x1_stats_ready")
        x1_meanvar_ready = sem("x1_meanvar_ready")
        ln_step = sem("ln_step")
        ln_ready = sem("ln_ready")
        xn_ready = sem("xn_ready")
        xt_filled = sem("xt_filled")
        xt_hi_ready = sem("xt_hi_ready")
        xt_lo_ready = sem("xt_lo_ready")
        half_scores_ready = sem("half_scores_ready")
        half_max_ready = sem("half_max_ready")
        half_shifted_ready = sem("half_shifted_ready")
        half_exp_ready = sem("half_exp_ready")
        half_sum_ready = sem("half_sum_ready")
        half_inv_ready = sem("half_inv_ready")
        half_probs_ready = sem("half_probs_ready")
        scores_ready = sem("scores_ready")
        row_max_ready = sem("row_max_ready")
        shifted_ready = sem("shifted_ready")
        exp_ready = sem("exp_ready")
        row_sum_ready = sem("row_sum_ready")
        row_inv_ready = sem("row_inv_ready")
        probs_ready = sem("probs_ready")
        pt_filled = sem("pt_filled")
        pt_hi_ready = sem("pt_hi_ready")
        pt_lo_ready = sem("pt_lo_ready")
        attn_ready = sem("attn_ready")
        x1_ready = sem("x1_ready")
        piece_maxed = sem("piece_maxed")
        piece_cast = sem("piece_cast")
        tmp_ready = sem("tmp_ready")
        piece_scaled = sem("piece_scaled")
        piece_split = sem("piece_split")
        xn2_ready = sem("xn2_ready")
        x2t_filled = sem("x2t_filled")
        x2t_hi_ready = sem("x2t_hi_ready")
        x2t_lo_ready = sem("x2t_lo_ready")
        gate_filled = sem("gate_filled")
        up_filled = sem("up_filled")
        silu_ready = sem("silu_ready")
        hidden_ready = sem("hidden_ready")
        h_hi_ready = sem("h_hi_ready")
        h_lo_ready = sem("h_lo_ready")
        down_filled = sem("down_filled")
        down_scaled = sem("down_scaled")
        out_ready = sem("out_ready")
        half_down_filled = sem("half_down_filled")
        half_down_scaled = sem("half_down_scaled")
        half_out_ready = sem("half_out_ready")

        order = ["kr0", "kr1", "u0", "u1", "u2", "a1_0", "u3", "t2_0", "t2_1"]
        order += [f"v{v}" for v in range(PAIRS - 1)] + ["a1_1", f"v{PAIRS - 1}", "t2_2", "t2_3"]
        order += [f"v{v}" for v in range(PAIRS, 2 * PAIRS)] + [f"g{h}" for h in range(H)]

        def slot_of(stage, n):
            return slot(order.index(f"{stage}{n}"))

        def v_part(s, v):
            return v_all[:, v // 2, s, v % 2 * 2:v % 2 * 2 + 2].rearrange("p b n -> p (b n)")

        def by_head(a):
            return a.rearrange("p (h l) -> p h l", h=H)

        def ex_half(n):
            return ex[0][:, n * HL // 2:(n + 1) * HL // 2]

        def x_tile(t):
            return x_res[:, bass.ds(t, 1), :].rearrange("p a n -> p (a n)")

        block = ctx.enter_context(nc.Block())

        @block.sync
        def _(sp):
            sp.dma_start(ctx_t, ctx_d).then_inc(ctx_loaded, 16)
            sp.dma_start(cos_t, cos_d).then_inc(ctx_loaded, 16)
            for q in range(2):
                half = slice(q * H * R // 2, (q + 1) * H * R // 2)
                sp.dma_start(wkr[:, half], wkr_d[:, half]).then_inc(wkr_loaded[q], 16)
            sp.dma_start(wkckv, wkckv_d).then_inc(wkckv_loaded, 16)

            def load_keys(g):
                sp.dma_start(wqr[:, 4 * g:4 * g + 4], wqr_d[:, 4 * g:4 * g + 4]).then_inc(keys_loaded[g], 16)
                sp.dma_start(wkcq[:, 4 * g:4 * g + 4], wkcq_d[:, 4 * g:4 * g + 4]).then_inc(keys_loaded[g], 16)

            load_keys(0)
            load_keys(1)
            for g, (h0, h1) in enumerate(WO_PARTS):
                sp.dma_start(wo[:, h0:h1], wo_d[:, h0:h1]).then_inc(wo_loaded[g], 16)
            load_keys(2)
            load_keys(3)
            sp.dma_start(gx[:, :], gx_d.partition_broadcast(P)).then_inc(params_loaded, 16)
            sp.dma_start(gf[:, :], gf_d.partition_broadcast(P)).then_inc(params_loaded, 16)
            sp.dma_start(sg[:, :], sg_d).then_inc(params_loaded, 16)
            sp.dma_start(su[:, :], su_d).then_inc(params_loaded, 16)
            sp.dma_start(down_row[:, :], sd_d.partition_broadcast(P)).then_inc(params_loaded, 16)
            for g in range(4):
                sp.dma_start(wq[:, 4 * g:4 * g + 4], wq_d[:, 4 * g:4 * g + 4]).then_inc(wq_loaded[g], 16)
            sp.wait_ge(g_scales_ready, 1)
            for t in range(TPB):
                sp.wait_ge(g_filled, t + 1)
                sp.dma_start(x_tile(t), x_d[:, t, :]).then_inc(first_x_loaded[t], 16)
            for g in range(1, B):
                sp.wait_ge(g_filled, 4 * g + 4)
                sp.dma_start(x_res[:, TPB * g:TPB * g + TPB], x_d[:, TPB * g:TPB * g + TPB]).then_inc(x_loaded[g], 16)

            def load_piece(m, r, wait=True):
                if wait:
                    sp.wait_ge(piece_cast, m * PPW + r - 1)
                    sp.wait_ge(piece_maxed, m * PPW + r - 1)
                sp.dma_start(staged(r), piece_source(m, r)).then_inc(piece_loaded[r % 2], 16)

            load_piece(0, 0, wait=False)
            load_piece(0, 1, wait=False)
            with sp.Fori(0, 2) as m:
                for r in range(2, PPW):
                    load_piece(m, r)
                for r in range(2):
                    load_piece(m + 1, r)
            for r in range(2, PPW):
                load_piece(2, r)
            sp.wait_ge(big_ready, 1)
            again = sp.value_load(big[0:1, 0:1], min_val=0, max_val=1)
            with sp.If(again != 0):
                for m in range(3):
                    for r in range(PPW):
                        n = m * PPW + r
                        if n >= 2:
                            sp.wait_ge(piece_split, n - 1)
                        sp.dma_start(staged_again(r), piece_source(m, r)).then_inc(piece_loaded[r % 2], 16)

            def store(b, i):
                sp.wait_ge(out_ready, b * TPB + i + 1)
                sp.dma_start(out_d[:, bass.ds(b * TPB + i, 1), :], o_sb[i].rearrange("p (a n) -> p a n", a=1)) \
                    .then_inc(out_stored[i], 16)

            with sp.Fori(0, B - 1) as b:
                for i in range(TPB):
                    store(b, i)
            for i in range(TPB - 1):
                store(B - 1, i)
            for ready, count, n in ((half_out_ready, 1, 0), (out_ready, NT, 1)):
                half = slice(n * D // 2, (n + 1) * D // 2)
                sp.wait_ge(ready, count)
                sp.dma_start(out_d[:, NT - 1, half], o_sb[TPB - 1][:, half]).then_inc(out_stored[TPB - 1], 16)
            for i in range(TPB):
                sp.wait_ge(out_stored[i], 16 * (B + 1 + (i == TPB - 1)))

        @block.gpsimd
        def _(pool):
            nc.gpsimd.memset(ident[:, :], 0.0).then_inc(pool_constants, 1)
            nc.gpsimd.memset(less_zero[:, :], -ZERO_POINT).then_inc(pool_constants, 1)
            pool.wait_ge(pool_constants, 2)
            nc.gpsimd.affine_select(out=ident[:, :], in_=ident[:, :], compare_op=ALU.not_equal, fill=1.0,
                                    base=0, pattern=[[-1, P]], channel_multiplier=1).then_inc(ident_ready, 1)
            for k0, k1 in ((0, 1), (1, 2), (2, 4)):
                pool.wait_ge(tensor_max, k1)
                nc.gpsimd.partition_all_reduce(all_max[:, k0:k1], tens_max[:, k0:k1], P, RMAX) \
                    .then_inc(max_shared, 1)

            def probabilities(i, m):
                pool.wait_ge(row_inv_ready, i + 1)
                nc.gpsimd.tensor_tensor(by_head(ex[m]), by_head(ex[m]),
                                        row_inv[:, m, :].unsqueeze(2).to_broadcast([P, H, L]), ALU.mult) \
                    .then_inc(probs_ready, 1)

            for n, inverted, ready in ((0, half_inv_ready, half_probs_ready), (1, row_inv_ready, probs_ready)):
                pool.wait_ge(inverted, 1)
                half = ex_half(n).rearrange("p (h l) -> p h l", h=H // 2)
                nc.gpsimd.tensor_tensor(half, half, row_inv[:, 0, n * H // 2:(n + 1) * H // 2].unsqueeze(2)
                                        .to_broadcast([P, H // 2, L]), ALU.mult).then_inc(ready, 1)
            for k in range(1, TPB):
                probabilities(k, k % 2)
            with pool.Fori(1, B) as g:
                for k in range(TPB):
                    probabilities(g * TPB + k, k % 2)
            pool.wait_ge(tensor_max, 6)
            nc.gpsimd.partition_all_reduce(all_max[:, 4:8], tens_max[:, 4:8], P, RMAX).then_inc(max_shared, 1)
            pool.wait_ge(big_ready, 1)
            again = pool.value_load(big[0:1, 0:1], min_val=0, max_val=1)
            with pool.If(again != 0):
                pool.wait_ge(attn_ready, NT)
                pool.wait_ge(ffn_scales_ready, 1)
                pool.wait_ge(piece_cast, PIECES)
                for n in range(PIECES):
                    m, r = n // PPW, n % PPW
                    w = piece_width(r)
                    pool.wait_ge(piece_loaded[r % 2], 16 * (PIECES // 2 + n // 2 + 1))
                    if n:
                        pool.wait_ge(piece_split, n)
                    nc.gpsimd.tensor_scalar(w_tmp[:, 0:w], staged_again(r), -ZERO_POINT, w_scale[:, m:m + 1],
                                            ALU.add, ALU.mult).then_inc(tmp_ready, 1)
                    pool.wait_ge(tmp_ready, n + 1)
                    nc.gpsimd.tensor_copy(w_hi(m, r), w_tmp[:, 0:w]).then_inc(piece_scaled, 1)
                    pool.wait_ge(piece_scaled, n + 1)
                    nc.gpsimd.tensor_tensor(w_lo(m, r), w_tmp[:, 0:w], w_hi(m, r), ALU.subtract) \
                        .then_inc(piece_split, 1)

        @block.scalar
        def _(act):
            act.dma_start(ctx_s, ctx_swapped_d).then_inc(ctx_loaded, 16)
            act.dma_start(sin_t, sin_d).then_inc(ctx_loaded, 16)
            squared = [0]

            def squares_of(w, loaded, parts, g):
                h0, h1 = parts[g]
                act.wait_ge(loaded[g], 16)
                if squared[0] > 0:
                    act.wait_ge(squares_ready, squared[0])
                nc.scalar.activation(junk[:, 0:(h1 - h0) * D], w[:, h0:h1, :].rearrange("p h n -> p (h n)"),
                                     ACT.Square, accum_out=part_sum[:, squared[0]:squared[0] + 1]) \
                    .then_inc(squares_ready, 1)
                squared[0] += 1

            for k in range(2):
                act.wait_ge(kr_filled, k + 1)
                nc.scalar.activation(krt[:, 4 * k:4 * k + 4, :].rearrange("p q n -> p (q n)"), slot_of("kr", k),
                                     ACT.Copy).then_inc(kr_copied, 1)
            for k in range(3):
                act.wait_ge(u_filled, k + 1)
                nc.scalar.activation(u_t[:, k * 1024:(k + 1) * 1024], slot_of("u", k), ACT.Copy) \
                    .then_inc(u_copied, 1)

            def copy_t2(k):
                act.wait_ge(t2_filled, k + 1)
                nc.scalar.activation(t2[:, k * 1024:(k + 1) * 1024], slot_of("t2_", k), ACT.Copy).then_inc(t2_copied, 1)

            def first_part_of_v(v):
                act.wait_ge(v_filled, v + 1)
                nc.scalar.activation(v_part(0, v), slot_of("v", v), ACT.Copy, scale=s1("v_up")).then_inc(v_hi_ready, 1)

            for g in range(len(WO_PARTS)):
                squares_of(wo, wo_loaded, WO_PARTS, g)
            act.wait_ge(v_scales_ready, 1)
            for v in range(PAIRS):
                first_part_of_v(v)
            squares_of(wq, wq_loaded, WQ_PARTS, 0)
            squares_of(wq, wq_loaded, WQ_PARTS, 1)
            copy_t2(2)
            copy_t2(3)
            for v in range(PAIRS, 2 * PAIRS):
                first_part_of_v(v)
                if v in (PAIRS + 1, PAIRS + 3):
                    squares_of(wq, wq_loaded, WQ_PARTS, 2 + (v - PAIRS - 1) // 2)
            act.wait_ge(params_loaded, 80)
            nc.scalar.activation(s1("tanh_x"), gx[:, :], ACT.Tanh).then_inc(tanh_ready, 1)
            nc.scalar.activation(s1("tanh_f"), gf[:, :], ACT.Tanh).then_inc(tanh_ready, 1)

            def normalise(dst, t):
                return nc.scalar.activation(dst, x_tile(t), ACT.Identity, scale=ln_scale[:, bass.ds(t, 1)],
                                            bias=ln_bias[:, bass.ds(t, 1)])

            def first_part_of_rows(t, k):
                act.wait_ge(xt_filled, t + 1)
                nc.scalar.activation(xt[:, k % 2, 0].rearrange("p c t -> p (c t)"), rows_ps(t), ACT.Copy) \
                    .then_inc(xt_hi_ready, 1)

            act.wait_ge(g_scales_ready, 1)
            for h in range(H):
                act.wait_ge(g_filled, h + 1)
                nc.scalar.activation(g_all[:, 0, :, :, h * L:(h + 1) * L].rearrange("p c b l -> p (c b) l"),
                                     slot_of("g", h).rearrange("p (m l) -> p m l", l=L),
                                     ACT.Copy, scale=s1("g_up")).then_inc(g_hi_ready, 1)
                if h == H - 4:
                    act.wait_ge(ln_ready, 1)
                    for t in range(2):
                        normalise(xn[t], t).then_inc(xn_ready, 1)
                if h == H - 2:
                    first_part_of_rows(0, 0)

            def attention_period(i, k, scores, probs, ln_count=None):
                if scores:
                    first_part_of_rows(i + 1, k + 1)
                    if isinstance(i, int) and i < 2:
                        normalise(xn[k % 2], i + 2).then_inc(xn_ready, 1)
                if probs:
                    act.wait_ge(pt_filled, i)
                    nc.scalar.activation(pt[:, (k + 1) % 2, 0].rearrange("p q t -> p (q t)"), pt_ps, ACT.Copy,
                                         scale=P_SCALE).then_inc(pt_hi_ready, 1)
                if scores and (not isinstance(i, int) or i >= 2):
                    if k == 2 and ln_count is not None:
                        act.wait_ge(ln_ready, ln_count)
                    normalise(xn[k % 2], (i + 2) % NT).then_inc(xn_ready, 1)
                if scores:
                    if isinstance(i, int) and i == 0:
                        for n, shifted, ready in ((0, half_shifted_ready, half_exp_ready),
                                                  (1, shifted_ready, exp_ready)):
                            act.wait_ge(shifted, 1)
                            nc.scalar.activation(ex_half(n), ex_half(n), ACT.Exp, scale=s1("exp_scale")) \
                                .then_inc(ready, 1)
                    else:
                        act.wait_ge(shifted_ready, i + 1)
                        nc.scalar.activation(ex[k % 2], ex[k % 2], ACT.Exp, scale=s1("exp_scale")) \
                            .then_inc(exp_ready, 1)

            def cast_pieces(m, k):
                for r in PIECES_OF_PERIOD[k]:
                    act.wait_ge(piece_loaded[r % 2], m * (16 * PPW // 2) + 16 * (r // 2 + 1))
                    nc.scalar.activation(w_hi(m, r), staged(r), ACT.Identity, scale=1.0, bias=less_zero[:, :]) \
                        .then_inc(piece_cast, 1)

            act.wait_ge(exp_scale_ready, 1)
            for k in range(TPB):
                attention_period(k, k, True, k >= 1, 2)
            act.wait_ge(pool_constants, 2)
            with act.Fori(1, B - 1) as g:
                for k in range(TPB):
                    attention_period(g * TPB + k, k, True, True, g + 2)
                    cast_pieces(g - 1, k)
            for k in range(TPB):
                attention_period((B - 1) * TPB + k, k, True, True)
                cast_pieces(B - 2, k)
                normalise(xn2[k], k).then_inc(xn2_ready, 1)

            def first_parts_of_x2t(b, ps):
                for i in range(TPB):
                    act.wait_ge(x2t_filled, b * TPB + i + 1)
                    nc.scalar.activation(x2t[:, 0, :, i * P:(i + 1) * P],
                                         ps(i).rearrange("p (c t) -> p c t", c=DCH), ACT.Copy) \
                        .then_inc(x2t_hi_ready, 1)

            attention_period(NT, 0, False, True)
            act.wait_ge(piece_cast, PIECES)
            act.wait_ge(piece_maxed, PIECES)
            first_parts_of_x2t(0, bank)
            act.wait_ge(ffn_scales_ready, 1)

            def batch(b, last):
                for j in range(JCH):
                    act.wait_ge(gate_filled, b * JCH + j + 1)
                    nc.scalar.activation(sil[j % 2], gate_ps(j), ACT.Silu, scale=sg[:, j:j + 1]) \
                        .then_inc(silu_ready, 1)
                    act.wait_ge(hidden_ready, b * JCH + j + 1)
                    nc.scalar.activation(h_all[:, 0, j, :], hid[j % 2], ACT.Copy).then_inc(h_hi_ready, 1)
                    if j in (1, 3, 5, 7) and not last:
                        if j == 1:
                            act.wait_ge(ln_ready, B + 2)
                        i = j // 2
                        normalise(xn2[i], b * TPB + TPB + i).then_inc(xn2_ready, 1)
                if not last:
                    first_parts_of_x2t(b + 1, x2t_ps)

            with act.Fori(0, B - 1) as b:
                batch(b, False)
            batch(B - 1, True)

        @block.vector
        def _(dve):
            dve.wait_ge(ctx_loaded, 64)

            def by_batch(a):
                return a.rearrange("p (b l) -> p b l", b=B)

            nc.vector.tensor_tensor(by_batch(kvt[:, :]), by_batch(ctx_t),
                                    cos_t.unsqueeze(1).to_broadcast([P, B, L]), ALU.mult).then_inc(rope_step, 1)
            nc.vector.tensor_tensor(by_batch(ctx_s), by_batch(ctx_s),
                                    sin_t.unsqueeze(1).to_broadcast([P, B, L]), ALU.mult).then_inc(rope_step, 1)
            dve.wait_ge(rope_step, 2)
            nc.vector.tensor_tensor(kvt[:, :], kvt[:, :], ctx_s, ALU.add).then_inc(kv_ready, 1)

            maxed = [0]

            def max_of(src):
                nc.vector.tensor_reduce(part_max[:, maxed[0]:maxed[0] + 1], src, AX.X, ALU.max,
                                        apply_absolute_value=True).then_inc(piece_max, 1)
                maxed[0] += 1

            def max_of_four(k):
                dve.wait_ge(piece_max, maxed[0])
                nc.vector.tensor_reduce(tens_max[:, k:k + 1], part_max[:, maxed[0] - 4:maxed[0]], AX.X, ALU.max) \
                    .then_inc(tensor_max, 1)

            steps = [0]

            def step(instruction):
                instruction.then_inc(sc_step, 1)
                steps[0] += 1
                dve.wait_ge(sc_step, steps[0])

            def sum_of_parts(k, k0, k1):
                dve.wait_ge(squares_ready, k1)
                nc.vector.tensor_reduce(tens_max[:, k:k + 1], part_sum[:, k0:k1], AX.X, ALU.add) \
                    .then_inc(tensor_max, 1)

            def fold_bound(first):
                step(nc.vector.tensor_scalar(s1("t0"), all_max[:, first:first + 1], all_max[:, first:first + 1],
                                             float(DK) ** 2, ALU.mult, ALU.mult))

            def fold_scales(first, up, ready):
                squares, t0, t1 = all_max[:, first + 1:first + 2], s1("t0"), s1("t1")
                step(nc.vector.tensor_scalar(t0, t0, squares, TINY, ALU.mult, ALU.max))
                step(nc.vector.tensor_scalar(t1.bitcast(INT32), t0.bitcast(INT32), 1, None, ALU.logical_shift_right))
                step(nc.vector.tensor_scalar(t1.bitcast(INT32), t1.bitcast(INT32), -1.0, float(0x5F3759DF),
                                             ALU.mult, ALU.add))
                nc.vector.tensor_scalar(s1(up), t1, 0.9 * TOP, None, ALU.mult).then_inc(ready, 1)
                dve.wait_ge(ready, 1)
                step(nc.vector.reciprocal(t1, s1(up)))

            def max_of_u(k):
                dve.wait_ge(u_copied, k + 1)
                max_of(u_t[:, k * 1024:(k + 1) * 1024])

            def copy_a1(k):
                dve.wait_ge(a1_filled, k + 1)
                nc.vector.tensor_copy(a1t[:, 4 * k:4 * k + 4].rearrange("p q k -> p (q k)"),
                                      slot_of("a1_", k)[:, 0:512]).then_inc(a1_copied, 1)

            def max_of_t2(k):
                dve.wait_ge(t2_copied, k + 1)
                max_of(t2[:, k * 1024:(k + 1) * 1024])

            def second_part_of_v(v):
                dve.wait_ge(v_hi_ready, v + 1)
                if v == 2 * PAIRS - 2:
                    dve.wait_ge(v_filled, v + 2)
                nc.vector.scalar_tensor_tensor(out=v_part(1, v), in0=slot_of("v", v), scalar=s1("v_up"),
                                               in1=v_part(0, v), op0=ALU.mult, op1=ALU.subtract) \
                    .then_inc(v_lo_ready, 1)

            max_of_u(0)
            max_of_u(1)
            copy_a1(0)
            max_of_u(2)
            dve.wait_ge(u_filled, 4)
            dve.wait_ge(u_copied, 3)
            nc.vector.tensor_copy(u_t[:, 3 * 1024:4 * 1024], slot_of("u", 3)).then_inc(u_copied, 1)
            max_of_u(3)
            max_of_four(0)
            for k in range(2):
                dve.wait_ge(t2_filled, k + 1)
                nc.vector.tensor_copy(t2[:, k * 1024:(k + 1) * 1024], slot_of("t2_", k)).then_inc(t2_copied, 1)
            dve.wait_ge(max_shared, 1)
            fold_bound(0)
            sum_of_parts(1, 0, len(WO_PARTS))
            dve.wait_ge(max_shared, 2)
            fold_scales(0, "v_up", v_scales_ready)
            step(nc.vector.tensor_scalar(s1("v_down"), s1("t1"), 1.0 / P_SCALE, None, ALU.mult))

            for v in range(PAIRS):
                second_part_of_v(v)
                if v == PAIRS - 2:
                    copy_a1(1)
            for k in range(3):
                max_of_t2(k)
            for v in range(PAIRS, 2 * PAIRS):
                second_part_of_v(v)
                if v == PAIRS + 1:
                    max_of_t2(3)
                    max_of_four(2)
                if v == PAIRS + 4:
                    sum_of_parts(3, len(WO_PARTS), len(WO_PARTS) + len(WQ_PARTS))
                if v == PAIRS + 5:
                    dve.wait_ge(max_shared, 3)
                    fold_bound(2)
                    fold_scales(2, "g_up", g_scales_ready)
                    nc.vector.tensor_scalar(s1("exp_scale"), s1("t1"), 1.0 / X_SCALE, None, ALU.mult) \
                        .then_inc(exp_scale_ready, 1)
            dve.wait_ge(tanh_ready, 2)
            step(nc.vector.tensor_tensor(s1("attn_gain"), s1("tanh_x"), s1("v_down"), ALU.mult))

            NEWTONS = 3
            LN_STEPS = 3 + 4 * NEWTONS + 1

            def normalisation(call, sets, scale, bias, stages=range(NEWTONS + 2)):
                v, y, c = (newton[:, m, sets, :] for m in range(3))
                mean = meanvar[:, sets, :, 0:1].rearrange("p s t a -> p s (t a)")
                var = meanvar[:, sets, :, 1:2].rearrange("p s t a -> p s (t a)")
                for stage in stages:
                    done = [0 if stage == 0 else 3 + 4 * (stage - 1)]

                    def after(instruction):
                        instruction.then_inc(ln_step, 1)
                        done[0] += 1
                        dve.wait_ge(ln_step, call * LN_STEPS + done[0])

                    if stage == 0:
                        after(nc.vector.tensor_scalar(v, var, EPS, None, ALU.add))
                        after(nc.vector.tensor_scalar(y.bitcast(INT32), v.bitcast(INT32), 1, None,
                                                      ALU.logical_shift_right))
                        after(nc.vector.tensor_scalar(y.bitcast(INT32), y.bitcast(INT32), -1.0, float(0x5F3759DF),
                                                      ALU.mult, ALU.add))
                    elif stage <= NEWTONS:
                        after(nc.vector.tensor_tensor(c, y, y, ALU.mult))
                        after(nc.vector.tensor_tensor(c, c, v, ALU.mult))
                        after(nc.vector.tensor_scalar(c, c, -0.5, 1.5, ALU.mult, ALU.add))
                        after(nc.vector.tensor_tensor(y, y, c, ALU.mult))
                    else:
                        after(nc.vector.tensor_scalar(scale, y, X_SCALE, None, ALU.mult))
                        nc.vector.scalar_tensor_tensor(out=bias, in0=mean, scalar=-1.0, in1=scale,
                                                       op0=ALU.mult, op1=ALU.mult).then_inc(ln_ready, 1)

            def of_batch(a, b):
                return a[:, bass.ds(b * TPB, TPB)].unsqueeze(1)

            def of_batches(a, b):
                return a[:, bass.ds(b * TPB, 3 * TPB)].rearrange("p (s t) -> p s t", s=3)[:, 0:3:2, :]

            def hold():
                dve.wait_ge(params_loaded, 80)

            def x_statistics(t, m, done, count):
                nc.vector.bn_stats(x_stats[:, m, :], x_tile(t)).then_inc(done, 1)
                hold()
                dve.wait_ge(done, count)
                nc.vector.bn_aggr(meanvar[:, 1, m, :], x_stats[:, m, :]).then_inc(meanvar_ready, 1)

            def first_normalisation(stages):
                normalisation(0, slice(1, 2), of_batch(ln_scale, 0), of_batch(ln_bias, 0), stages)

            def second_part_of_rows(i, k):
                dve.wait_ge(xt_hi_ready, i + 1)
                nc.vector.tensor_tensor(xt[:, k % 2, 1].rearrange("p c t -> p (c t)"), rows_ps(i),
                                        xt[:, k % 2, 0].rearrange("p c t -> p (c t)"),
                                        ALU.subtract).then_inc(xt_lo_ready, 1)

            for h in range(H):
                dve.wait_ge(g_hi_ready, h + 1)
                nc.vector.scalar_tensor_tensor(
                    out=g_all[:, 1, :, :, h * L:(h + 1) * L].rearrange("p c b l -> p (c b) l"),
                    in0=slot_of("g", h).rearrange("p (m l) -> p m l", l=L), scalar=s1("g_up"),
                    in1=g_all[:, 0, :, :, h * L:(h + 1) * L].rearrange("p c b l -> p (c b) l"),
                    op0=ALU.mult, op1=ALU.subtract).then_inc(g_lo_ready, 1)
                if 2 <= h < 2 + TPB:
                    dve.wait_ge(first_x_loaded[h - 2], 16)
                    x_statistics(h - 2, h - 2, stats_ready, h - 1)
                elif h == 6:
                    dve.wait_ge(meanvar_ready, TPB)
                    first_normalisation([0])
                elif h in (7, 8):
                    first_normalisation([h - 6])
                elif h == 9:
                    first_normalisation([3, 4])
                elif h == H - 2:
                    second_part_of_rows(0, 0)

            def first_tile():
                hh = H // 2
                for n, scores, maxed, shifted in (
                        (0, half_scores_ready, half_max_ready, half_shifted_ready),
                        (1, scores_ready, row_max_ready, shifted_ready)):
                    half = scores_ps(0)[:, n * 512:(n + 1) * 512].rearrange("p (h l) -> p h l", h=hh)
                    rows = row_max[:, 0, n * hh:(n + 1) * hh]
                    dve.wait_ge(scores, 1)
                    nc.vector.tensor_reduce(rows, half, AX.X, ALU.max).then_inc(maxed, 1)
                    dve.wait_ge(maxed, 1)
                    nc.vector.tensor_tensor(ex_half(n).rearrange("p (h l) -> p h l", h=hh), half,
                                            rows.unsqueeze(2).to_broadcast([P, hh, L]), ALU.subtract) \
                        .then_inc(shifted, 1)
                for n, exped, summed, inverted in ((0, half_exp_ready, half_sum_ready, half_inv_ready),
                                                   (1, exp_ready, row_sum_ready, row_inv_ready)):
                    rows = slice(n * hh, (n + 1) * hh)
                    dve.wait_ge(exped, 1)
                    nc.vector.tensor_reduce(row_sum[:, 0, rows], ex_half(n).rearrange("p (h l) -> p h l", h=hh),
                                            AX.X, ALU.add).then_inc(summed, 1)
                    dve.wait_ge(summed, 1)
                    nc.vector.reciprocal(row_inv[:, 0, rows], row_sum[:, 0, rows]).then_inc(inverted, 1)

            def attention_period(i, k, scores, probs, attn):
                m = k % 2
                if scores:
                    second_part_of_rows(i + 1, k + 1)
                if scores and isinstance(i, int) and i == 0:
                    first_tile()
                    return
                if scores:
                    dve.wait_ge(scores_ready, i + 1)
                    nc.vector.tensor_reduce(row_max[:, m, :], by_head(scores_ps(k)), AX.X, ALU.max) \
                        .then_inc(row_max_ready, 1)
                    dve.wait_ge(row_max_ready, i + 1)
                    nc.vector.tensor_tensor(by_head(ex[m]), by_head(scores_ps(k)),
                                            row_max[:, m, :].unsqueeze(2).to_broadcast([P, H, L]),
                                            ALU.subtract).then_inc(shifted_ready, 1)
                if probs:
                    dve.wait_ge(pt_hi_ready, i)
                    nc.vector.scalar_tensor_tensor(out=pt[:, (k + 1) % 2, 1].rearrange("p q t -> p (q t)"),
                                                   in0=pt_ps, scalar=P_SCALE,
                                                   in1=pt[:, (k + 1) % 2, 0].rearrange("p q t -> p (q t)"),
                                                   op0=ALU.mult, op1=ALU.subtract).then_inc(pt_lo_ready, 1)
                if scores:
                    dve.wait_ge(exp_ready, i + 1)
                    nc.vector.tensor_reduce(row_sum[:, m, :], by_head(ex[m]), AX.X, ALU.add) \
                        .then_inc(row_sum_ready, 1)
                    dve.wait_ge(row_sum_ready, i + 1)
                    nc.vector.reciprocal(row_inv[:, m, :], row_sum[:, m, :]).then_inc(row_inv_ready, 1)
                if attn:
                    dve.wait_ge(attn_ready, i - 1)
                    nc.vector.scalar_tensor_tensor(out=x_tile(i - 2), in0=out_ps, scalar=s1("attn_gain"),
                                                   in1=x_tile(i - 2), op0=ALU.mult, op1=ALU.add) \
                        .then_inc(x1_ready, 1)
                    hold()
                    dve.wait_ge(x1_ready, i - 1)
                    nc.vector.bn_stats(x1_stats[:, (k + 2) % TPB, :], x_tile(i - 2)).then_inc(x1_stats_ready, 1)
                    hold()
                    dve.wait_ge(x1_stats_ready, i - 1)
                    nc.vector.bn_aggr(meanvar[:, 0, (k + 2) % TPB, :], x1_stats[:, (k + 2) % TPB, :]) \
                        .then_inc(x1_meanvar_ready, 1)

            def maxima_of_pieces(m, k):
                for r in PIECES_OF_PERIOD[k]:
                    dve.wait_ge(piece_loaded[r % 2], m * (16 * PPW // 2) + 16 * (r // 2 + 1))
                    nc.vector.tensor_reduce(ffn_max[:, bass.ds(m * PPW + r, 1)], staged(r), AX.X, ALU.max,
                                            apply_absolute_value=True).then_inc(piece_maxed, 1)

            def next_statistics(g, k):
                if k < 2:
                    for m in (2 * k, 2 * k + 1):
                        if isinstance(g, int):
                            x_statistics((g + 1) * TPB + m, m, stats_ready, (g + 1) * TPB + m + 1)
                        else:
                            x_statistics((g + 1) * TPB + m, m, late_stats_ready[m], g)

            for k in range(TPB):
                attention_period(k, k, True, k >= 1, k >= 2)
                if k == 0:
                    dve.wait_ge(x_loaded[1], 16)
                next_statistics(0, k)
                if k == 1:
                    dve.wait_ge(meanvar_ready, 2 * TPB)
                    normalisation(1, slice(1, 2), of_batch(ln_scale, 1), of_batch(ln_bias, 1))
            for g in range(2, B):
                dve.wait_ge(x_loaded[g], 16)
            with dve.Fori(1, B - 1) as g:
                for k in range(TPB):
                    attention_period(g * TPB + k, k, True, True, True)
                    next_statistics(g, k)
                    if k == 1:
                        dve.wait_ge(x1_meanvar_ready, g * TPB)
                        dve.wait_ge(meanvar_ready, g * TPB + 2 * TPB)
                        normalisation(g + 1, slice(0, 2), of_batches(ln_scale, g - 1), of_batches(ln_bias, g - 1))
                    maxima_of_pieces(g - 1, k)
            for k in range(TPB):
                attention_period((B - 1) * TPB + k, k, True, True, True)
                if k == 1:
                    dve.wait_ge(x1_meanvar_ready, (B - 1) * TPB)
                    normalisation(B, slice(0, 1), of_batch(ln_scale, B - 2), of_batch(ln_bias, B - 2))
                maxima_of_pieces(B - 2, k)

            def second_parts_of_x2t(b, ps):
                for i in range(TPB):
                    dve.wait_ge(x2t_hi_ready, b * TPB + i + 1)
                    nc.vector.tensor_tensor(x2t[:, 1, :, i * P:(i + 1) * P],
                                            ps(i).rearrange("p (c t) -> p c t", c=DCH),
                                            x2t[:, 0, :, i * P:(i + 1) * P], ALU.subtract) \
                        .then_inc(x2t_lo_ready, 1)

            attention_period(NT, 0, False, True, False)
            second_parts_of_x2t(0, bank)
            attention_period(NT, 0, False, False, True)

            step(nc.vector.tensor_tensor(sgsu[:, :], sg[:, :], su[:, :], ALU.mult))
            nc.vector.tensor_reduce(tens_max[:, 7:8], sgsu[:, :], AX.X, ALU.max,
                                    apply_absolute_value=True).then_inc(tensor_max, 1)
            dve.wait_ge(piece_maxed, PIECES)
            nc.vector.tensor_reduce(tens_max[:, 4:7], ffn_max[:, :].rearrange("p (m n) -> p m n", m=3),
                                    AX.X, ALU.max).then_inc(tensor_max, 1)
            dve.wait_ge(max_shared, 4)
            step(nc.vector.tensor_scalar(w_big, all_max[:, 4:7], EXACT - ZERO_POINT, None, ALU.is_gt))
            step(nc.vector.tensor_reduce(s1("t0"), w_big, AX.X, ALU.max))
            nc.vector.tensor_copy(big[:, :], s1("t0")).then_inc(big_ready, 1)
            step(nc.vector.tensor_scalar(w_bound, all_max[:, 4:7], ZERO_POINT, None, ALU.add))
            step(nc.vector.reciprocal(w_scale, w_bound))
            step(nc.vector.tensor_scalar(w_scale, w_scale, EXACT, 1.0, ALU.mult, ALU.subtract))
            step(nc.vector.tensor_tensor(w_scale, w_scale, w_big, ALU.mult))
            step(nc.vector.tensor_scalar(w_scale, w_scale, 1.0, None, ALU.add))
            step(nc.vector.reciprocal(w_inv, w_scale))
            step(nc.vector.tensor_tensor(s1("t0"), w_bound[:, 0:1], w_bound[:, 1:2], ALU.mult))
            step(nc.vector.tensor_tensor(s1("t0"), s1("t0"), all_max[:, 7:8], ALU.mult))
            step(nc.vector.tensor_scalar(s1("h_bound"), s1("t0"), float(D) * D, TINY, ALU.mult, ALU.max))
            step(nc.vector.reciprocal(s1("t1"), s1("h_bound")))
            step(nc.vector.tensor_scalar(s1("gate_k"), w_inv[:, 0:1], 1.0 / X_SCALE, None, ALU.mult))
            step(nc.vector.tensor_scalar(s1("up_k"), w_inv[:, 1:2], s1("t1"), TOP / X_SCALE, ALU.mult, ALU.mult))
            step(nc.vector.tensor_scalar(s1("down_k"), w_inv[:, 2:3], s1("h_bound"), 1.0 / TOP, ALU.mult, ALU.mult))
            step(nc.vector.tensor_tensor(s1("down_k"), s1("down_k"), s1("tanh_f"), ALU.mult))
            step(nc.vector.tensor_scalar(sg[:, :], sg[:, :], s1("gate_k"), None, ALU.mult))
            step(nc.vector.tensor_scalar(su[:, :], su[:, :], s1("up_k"), None, ALU.mult))
            nc.vector.tensor_scalar(down_row[:, :], down_row[:, :], s1("down_k"), None, ALU.mult) \
                .then_inc(ffn_scales_ready, 1)

            attention_period(NT + 1, 1, False, False, True)
            dve.wait_ge(x1_meanvar_ready, NT)
            normalisation(B + 1, slice(0, 1), of_batch(ln_scale, B - 1), of_batch(ln_bias, B - 1))
            for i in range(TPB):
                dve.sem_inc(out_stored[i], 16)
            dve.wait_ge(ffn_scales_ready, 1)

            def batch(b, last):
                for j in range(JCH):
                    dve.wait_ge(up_filled, b * JCH + j + 1)
                    dve.wait_ge(silu_ready, b * JCH + j + 1)
                    nc.vector.scalar_tensor_tensor(out=hid[j % 2], in0=up_ps(j), scalar=su[:, j:j + 1],
                                                   in1=sil[j % 2], op0=ALU.mult, op1=ALU.mult) \
                        .then_inc(hidden_ready, 1)
                    dve.wait_ge(h_hi_ready, b * JCH + j + 1)
                    nc.vector.tensor_tensor(h_all[:, 1, j, :], hid[j % 2], h_all[:, 0, j, :], ALU.subtract) \
                        .then_inc(h_lo_ready, 1)
                if not last:
                    second_parts_of_x2t(b + 1, x2t_ps)
                for i in range(TPB - last):
                    dve.wait_ge(down_filled, b * TPB + i + 1)
                    dve.wait_ge(out_stored[i], 16 * (b + 1))
                    nc.vector.tensor_tensor(o_sb[i], down_ps(i), down_row[:, :], ALU.mult).then_inc(down_scaled, 1)
                    dve.wait_ge(down_scaled, b * TPB + i + 1)
                    nc.vector.tensor_tensor(o_sb[i], o_sb[i], x_tile(b * TPB + i), ALU.add).then_inc(out_ready, 1)

            with dve.Fori(0, B - 1) as b:
                batch(b, False)
            batch(B - 1, True)
            i = TPB - 1
            dve.wait_ge(out_stored[i], 16 * B)
            for filled, scaled, ready, n in ((half_down_filled, half_down_scaled, half_out_ready, 0),
                                             (down_filled, down_scaled, out_ready, 1)):
                half = slice(n * D // 2, (n + 1) * D // 2)
                count = NT if n else 1
                dve.wait_ge(filled, count)
                nc.vector.tensor_tensor(o_sb[i][:, half], last_ps(n)[:, half], down_row[:, half], ALU.mult) \
                    .then_inc(scaled, 1)
                dve.wait_ge(scaled, count)
                nc.vector.tensor_tensor(o_sb[i][:, half], o_sb[i][:, half], x_tile(NT - 1)[:, half], ALU.add) \
                    .then_inc(ready, 1)

        @block.tensor
        def _(pe):
            pe.wait_ge(ident_ready, 1)
            for _ in range(WARM_UPS):
                nc.tensor.transpose(pt_ps[:, 0:P], ident[:, :], ident[:, :])
            pe.wait_ge(kv_ready, 1)
            for q in range(PAIRS):
                if q % 4 == 0:
                    pe.wait_ge(wkr_loaded[q // 4], 16)
                last = nc.tensor.matmul(slot_of("kr", q // 4)[:, q % 4 * BL:(q % 4 + 1) * BL],
                                        wkr[:, q * P:(q + 1) * P], kvt[:, :], start=True, stop=True)
                if q % 4 == 3:
                    last.then_inc(kr_filled, 1)
            def make_u(k):
                for h in range(4 * k, 4 * k + 4):
                    last = nc.tensor.matmul(slot_of("u", k)[:, (h % 4) * BL:(h % 4 + 1) * BL],
                                            wkckv[:, h * DK:(h + 1) * DK], kvt[:, :], start=True, stop=True)
                last.then_inc(u_filled, 1)

            def make_a1(k):
                for q in range(4 * k, 4 * k + 4):
                    if q % 2 == 0:
                        pe.wait_ge(keys_loaded[q // 2], 32)
                    for c in range(QCH):
                        for h in (2 * q, 2 * q + 1):
                            half = (h % 2) * R
                            last = nc.tensor.matmul(slot_of("a1_", k)[half:half + R, q % 4 * DK:(q % 4 + 1) * DK],
                                                    wqr[:, h, c, :], wkcq[:, h, c, :],
                                                    start=c == 0, stop=c == QCH - 1)
                last.then_inc(a1_filled, 1)

            def make_t2(k):
                for h in range(4 * k, 4 * k + 4):
                    half = (h % 2) * R
                    at_h = (t2_at(h) % 4) * BL
                    last = nc.tensor.matmul(slot_of("t2_", k)[:, at_h:at_h + BL], a1t[half:half + R, h // 2, :],
                                            krt[half:half + R, h // 2, :], start=True, stop=True)
                last.then_inc(t2_filled, 1)

            def make_v(v):
                q = v // 2
                if v % 2 == 0 and 2 * q in (h0 for h0, _ in WO_PARTS):
                    pe.wait_ge(wo_loaded[[h0 for h0, _ in WO_PARTS].index(2 * q)], 16)
                for m in range(2):
                    b = v % 2 * 2 + m
                    for h in (2 * q, 2 * q + 1):
                        half = (h % 2) * L
                        at_u = h * BL + b * L
                        last = nc.tensor.matmul(slot_of("v", v)[half:half + L, m * D:(m + 1) * D],
                                                u_t[:, at_u:at_u + L], wo[:, h, :], start=True, stop=True)
                last.then_inc(v_filled, 1)

            pe.wait_ge(wkckv_loaded, 16)
            make_u(0)
            make_u(1)
            pe.wait_ge(kr_copied, 1)
            make_u(2)
            pe.wait_ge(kr_copied, 2)
            make_a1(0)
            pe.wait_ge(u_copied, 1)
            make_u(3)
            pe.wait_ge(a1_copied, 1)
            for k in range(2):
                pe.wait_ge(u_copied, k + 2)
                make_t2(k)
            for v in range(PAIRS - 1):
                if v == 0:
                    pe.wait_ge(u_copied, 4)
                elif v in (2, 3):
                    pe.wait_ge(t2_copied, v - 1)
                elif v > 3:
                    pe.wait_ge(v_lo_ready, v - 3)
                make_v(v)
            pe.wait_ge(v_lo_ready, PAIRS - 4)
            make_a1(1)
            pe.wait_ge(v_lo_ready, PAIRS - 3)
            make_v(PAIRS - 1)
            pe.wait_ge(a1_copied, 2)
            for k in range(2, 4):
                pe.wait_ge(v_lo_ready, PAIRS - 4 + k)
                make_t2(k)
            for v in range(PAIRS, 2 * PAIRS):
                if v == PAIRS + 1:
                    pe.wait_ge(v_lo_ready, PAIRS)
                elif v in (PAIRS + 2, PAIRS + 3):
                    pe.wait_ge(t2_copied, v - PAIRS + 1)
                elif v > PAIRS + 3:
                    pe.wait_ge(v_lo_ready, v - 3)
                make_v(v)
            def transpose_rows(dst, src):
                for c in range(DCH):
                    last = nc.tensor.transpose(dst[:, c * P:(c + 1) * P], src[:, c * P:(c + 1) * P], ident[:, :])
                return last

            for h in range(H):
                if h == H - 1:
                    pe.wait_ge(xn_ready, 2)
                    pe.wait_ge(g_lo_ready, H - 3)
                    for t in range(2):
                        transpose_rows(rows_ps(t), xn[t]).then_inc(xt_filled, 1)
                if h % 4 == 0:
                    pe.wait_ge(wq_loaded[h // 4], 16)
                if h < 4:
                    pe.wait_ge(v_lo_ready, 2 * PAIRS - 3 + h)
                else:
                    pe.wait_ge(g_lo_ready, h - 3)
                for c in range(DCH):
                    last = nc.tensor.matmul(slot_of("g", h)[:, c * BL:(c + 1) * BL], wq[:, h, c * P:(c + 1) * P],
                                            t2[:, t2_at(h) * BL:(t2_at(h) + 1) * BL], start=True, stop=True)
                last.then_inc(g_filled, 1)

            def g_at(s, c, b, n):
                return g_region[:, bass.ds((s * DCH + c) * B * HL + b * HL + n * 512, 512)]

            def v_at(q, s, b):
                return v_region[:, bass.ds((q * 2 + s) * B * D + b * D, D)]

            def attention_period(i, k, b, scores, probs, attn):
                if scores:
                    m = k % 2
                    if not (isinstance(i, int) and i == 0):
                        pe.wait_ge(xn_ready, i + 2)
                    pe.wait_ge(xt_lo_ready, i + 1)
                    if not (isinstance(i, int) and i == 0):
                        transpose_rows(xt_ps, xn[(k + 1) % 2]).then_inc(xt_filled, 1)
                    if not isinstance(i, int) or i >= 2:
                        pe.wait_ge(shifted_ready, i - 1)
                    if isinstance(i, int) and i == 0:
                        pe.wait_ge(g_lo_ready, H - 2)
                        for n in range(HL // 512):
                            if n == 1:
                                last.then_inc(half_scores_ready, 1)
                                pe.wait_ge(g_lo_ready, H)
                            for c in range(DCH):
                                for sx, sy in ((0, 0), (0, 1), (1, 0)):
                                    last = nc.tensor.matmul(scores_ps(k)[:, n * 512:(n + 1) * 512],
                                                            xt[:, m, sx, c, :], g_at(sy, c, b, n),
                                                            start=c == 0 and sx + sy == 0,
                                                            stop=c == DCH - 1 and sx == 1)
                    else:
                        for c in range(DCH):
                            for sx, sy in ((0, 0), (0, 1), (1, 0)):
                                for n in range(HL // 512):
                                    last = nc.tensor.matmul(scores_ps(k)[:, n * 512:(n + 1) * 512],
                                                            xt[:, m, sx, c, :], g_at(sy, c, b, n),
                                                            start=c == 0 and sx + sy == 0,
                                                            stop=c == DCH - 1 and sx == 1)
                    last.then_inc(scores_ready, 1)
                if probs:
                    if isinstance(i, int) and i == 1:
                        pe.wait_ge(half_probs_ready, 1)
                    pe.wait_ge(probs_ready, i)
                    if not isinstance(i, int) or i >= 2:
                        pe.wait_ge(pt_lo_ready, i - 1)
                    for q in range(PAIRS):
                        last = nc.tensor.transpose(pt_ps[:, q * P:(q + 1) * P],
                                                   ex[(k + 1) % 2][:, q * P:(q + 1) * P], ident[:, :])
                    last.then_inc(pt_filled, 1)
                if attn:
                    pe.wait_ge(pt_lo_ready, i - 1)
                    if not isinstance(i, int) or i >= 3:
                        pe.wait_ge(x1_ready, i - 2)
                    bb = b if k % TPB >= 2 else b - 1
                    for q in range(PAIRS):
                        for sx, sy in ((0, 0), (0, 1), (1, 0)):
                            last = nc.tensor.matmul(out_ps, pt[:, k % 2, sx, q, :], v_at(q, sy, bb),
                                                    start=q == 0 and sx + sy == 0,
                                                    stop=q == PAIRS - 1 and sx == 1)
                    last.then_inc(attn_ready, 1)

            for k in range(TPB):
                attention_period(k, k, 0, True, k >= 1, k >= 2)
            with pe.Fori(1, B) as g:
                for k in range(TPB):
                    attention_period(g * TPB + k, k, g, True, True, True)

            def transpose_batch(b, ps):
                for i in range(TPB):
                    pe.wait_ge(xn2_ready, b * TPB + i + 1)
                    transpose_rows(ps(i), xn2[i]).then_inc(x2t_filled, 1)

            def feed_forward(parts):
                def batch(b, last):
                    pe.wait_ge(x2t_lo_ready, b * TPB + TPB)
                    for j in range(JCH):
                        for m, ps, filled, freed in ((0, gate_ps(j), gate_filled, silu_ready),
                                                     (1, up_ps(j), up_filled, hidden_ready)):
                            if j >= 2:
                                pe.wait_ge(freed, b * JCH + j - 1)
                            for c in range(DCH):
                                for sx, w in parts:
                                    done = nc.tensor.matmul(ps, columns(w, m, c * HID + j * P, P), x2t[:, sx, c, :],
                                                            start=c == 0 and (sx, w) == parts[0],
                                                            stop=c == DCH - 1 and (sx, w) == parts[-1])
                            done.then_inc(filled, 1)
                    if not last:
                        pe.wait_ge(silu_ready, b * JCH + JCH - 1)
                        pe.wait_ge(hidden_ready, b * JCH + JCH - 1)
                        transpose_batch(b + 1, x2t_ps)
                    pe.wait_ge(h_lo_ready, b * JCH + JCH - 1)
                    for i in range(TPB):
                        if i >= 2:
                            pe.wait_ge(down_scaled, b * TPB + i - 1)
                        halves = 2 if last and i == TPB - 1 else 1
                        for n in range(halves):
                            width = D // halves
                            for j in range(JCH):
                                if i == 0 and j == JCH - 1:
                                    pe.wait_ge(h_lo_ready, b * JCH + JCH)
                                for sx, w in parts:
                                    done = nc.tensor.matmul((last_ps(n) if halves == 2 else down_ps(i))
                                                            [:, n * width:(n + 1) * width],
                                                            h_all[:, sx, j, i * P:(i + 1) * P],
                                                            columns(w, 2, j * D + n * width, width),
                                                            start=j == 0 and (sx, w) == parts[0],
                                                            stop=j == JCH - 1 and (sx, w) == parts[-1])
                            done.then_inc(down_filled if n == halves - 1 else half_down_filled, 1)

                with pe.Fori(0, B - 1) as b:
                    batch(b, False)
                batch(B - 1, True)

            pe.wait_ge(shifted_ready, NT)
            transpose_batch(0, bank)
            attention_period(NT, 0, B, False, True, True)
            attention_period(NT + 1, 1, B, False, False, True)
            pe.wait_ge(pt_lo_ready, NT)
            pe.wait_ge(xt_lo_ready, NT + 1)
            pe.wait_ge(piece_cast, PIECES)
            pe.wait_ge(big_ready, 1)
            general = pe.value_load(big[0:1, 0:1], min_val=0, max_val=1)
            with pe.If(general != 0):
                pe.wait_ge(piece_split, PIECES)
                feed_forward([(0, w_hi), (0, w_lo), (1, w_hi)])
            with pe.Else():
                feed_forward([(0, w_hi), (1, w_hi)])


def kernel(x, ctx_512, g_xattn, g_ffn, L0_xattn_Wq, L0_xattn_w_kc_q, L0_xattn_w_kc_kv, L0_xattn_W_qr,
           L0_xattn_W_kr, L0_xattn_Wo, L0_ffn_wq_gate, L0_ffn_s_gate, L0_ffn_wq_up, L0_ffn_s_up,
           L0_ffn_wq_down, L0_ffn_s_down):
    import numpy as np
    import concourse.bacc as bacc
    from concourse.bass_utils import run_bass_kernel_spmd

    inv_freq = (1.0 / np.float32(10000.0) ** (np.arange(0, DC, 2, dtype=np.float32) / np.float32(DC)))
    freqs = np.arange(L, dtype=np.float32)[:, None] * inv_freq.astype(np.float32)[None, :]
    cos = np.repeat(np.cos(freqs), 2, axis=-1).T
    sin = np.repeat(np.sin(freqs), 2, axis=-1).T
    sign = np.where(np.arange(DC) < DC // 2, -1.0, 1.0).astype(np.float32)[:, None]

    a = {k: np.asarray(v) for k, v in dict(
        x=x, ctx=ctx_512, gx=g_xattn, gf=g_ffn, wq=L0_xattn_Wq, wkcq=L0_xattn_w_kc_q, wkckv=L0_xattn_w_kc_kv,
        wqr=L0_xattn_W_qr, wkr=L0_xattn_W_kr, wo=L0_xattn_Wo, wg=L0_ffn_wq_gate, wu=L0_ffn_wq_up,
        wd=L0_ffn_wq_down, sg=L0_ffn_s_gate, su=L0_ffn_s_up, sd=L0_ffn_s_down).items()}
    ctx_t = a["ctx"].reshape(BL, DC).T
    laid = [
        ("x", a["x"].reshape(NT, P, D).transpose(1, 0, 2)),
        ("ctx_t", ctx_t),
        ("ctx_swapped", np.concatenate([ctx_t[DC // 2:], ctx_t[:DC // 2]])),
        ("cos", cos.astype(np.float32)),
        ("sin", (sin * sign).astype(np.float32)),
        ("gx", a["gx"]),
        ("gf", a["gf"]),
        ("wq", a["wq"].reshape(H, DK, D).transpose(1, 0, 2)),
        ("wkcq", a["wkcq"].reshape(H, DK, QCH, P).transpose(3, 0, 2, 1)),
        ("wkckv", a["wkckv"].transpose(2, 0, 1).reshape(DC, H * DK)),
        ("wqr", a["wqr"].reshape(H, QCH, P, R).transpose(2, 0, 1, 3)),
        ("wkr", a["wkr"].transpose(1, 0, 2).reshape(DC, H * R)),
        ("wo", a["wo"].T.reshape(H, DK, D).transpose(1, 0, 2)),
        ("wffn", np.stack([a["wg"].T.reshape(DCH, P, HID).transpose(1, 0, 2).reshape(P, W_COLS),
                           a["wu"].T.reshape(DCH, P, HID).transpose(1, 0, 2).reshape(P, W_COLS),
                           a["wd"].T.reshape(JCH, P, D).transpose(1, 0, 2).reshape(P, W_COLS)], axis=1)),
        ("sg", a["sg"].reshape(JCH, P).T),
        ("su", a["su"].reshape(JCH, P).T),
        ("sd", a["sd"]),
    ]
    nc = bacc.Bacc("TRN2", target_bir_lowering=False, num_devices=1)
    arrays, aps = {}, []
    for name, v in laid:
        v = np.ascontiguousarray(v)
        arrays[f"in_{name}"] = v
        aps.append(nc.dram_tensor(f"in_{name}", v.shape, mybir.dt.from_np(v.dtype), kind="ExternalInput").ap())
    aps.append(nc.dram_tensor("out_0", (P, NT, D), FP32, kind="ExternalOutput").ap())
    gated_block(nc, *aps)
    r = run_bass_kernel_spmd(nc, [arrays], core_ids=[0])
    out = r.results[0]["out_0"]
    return np.ascontiguousarray(np.asarray(out).transpose(1, 0, 2)).reshape(B, S, D)
```
